# Optimizing a Trainium2 kernel written in Bass

```python
import numpy as np
import jax
import jax.numpy as jnp

def _softmax(x, axis=-1):
    return jax.nn.softmax(x, axis=axis)

def _gelu(x):
    return jax.nn.gelu(x, approximate=True)

def _silu(x):
    return jax.nn.silu(x)

def _sigmoid(x):
    return jax.nn.sigmoid(x)

def _layernorm(x, axis=-1, eps=1e-05):
    m = jnp.mean(x, axis=axis, keepdims=True)
    v = jnp.var(x, axis=axis, keepdims=True)
    return (x - m) / jnp.sqrt(v + eps)

def _scatter_add(tgt, idx, src, axis=0):
    return tgt.at[idx].add(src)

def _segment_sum(src, seg, n):
    return jax.ops.segment_sum(src, seg, n)
kernel_name = 'mk_adaln_d1_jaxref_r4_33bfbf'

def setup_inputs(seed: int=0):
    np.random.seed(seed)
    _w = jnp.asarray

    def _L0_attn_setup():
        import jax, jax.numpy as jnp
        import numpy as np
        EPS = 1.1920929e-07

        def _rms(x):
            return x * jax.lax.rsqrt(jnp.mean(x * x, axis=-1, keepdims=True) + EPS)
        key = jax.random.key(seed)
        k0, k1, k2, k3 = jax.random.split(key, 4)
        B, S, D, DFF = (4, 512, 512, 2048)
        x = jax.random.normal(k0, (B, S, D), dtype=jnp.float32)
        w_qkv = jax.random.normal(k1, (3 * D, D), dtype=jnp.float32) * 0.02
        w_swiglu = jax.random.normal(k2, (2 * DFF, D), dtype=jnp.float32) * 0.02
        w_out = jax.random.normal(k3, (D, DFF), dtype=jnp.float32) * 0.02
        return {'x': x, 'w_qkv': w_qkv, 'w_swiglu': w_swiglu, 'w_out': w_out}
    _L0_attn_in = _L0_attn_setup()

    def _L0_ffn_setup():
        import jax, jax.numpy as jnp
        import numpy as np
        K = 2

        def gelu(v):
            return jax.nn.gelu(v, approximate=False)
        key = jax.random.key(seed)
        ks = jax.random.split(key, 10)
        B, S, D, H, E = (4, 512, 512, 256, 8)
        SH = 2 * H
        u = lambda k_, shape, b: jax.random.uniform(k_, shape, jnp.float32, -b, b)
        return {'x': jax.random.normal(ks[0], (B, S, D), jnp.float32), 'gate_w': u(ks[1], (D, E), 1.0 / D), 'w1': u(ks[2], (E, D, H), 1.0 / D), 'b1': u(ks[3], (E, H), 1.0 / np.sqrt(D)), 'w2': u(ks[4], (E, H, D), 1.0 / H), 'b2': u(ks[5], (E, D), 1.0 / np.sqrt(H)), 'shared_w1': u(ks[6], (D, SH), 1.0 / D), 'shared_b1': u(ks[7], (SH,), 1.0 / np.sqrt(D)), 'shared_w2': u(ks[8], (SH, D), 1.0 / SH), 'shared_b2': u(ks[9], (D,), 1.0 / np.sqrt(SH))}
    _L0_ffn_in = _L0_ffn_setup()
    _L0_c = _w((lambda *s: np.random.randn(*s).astype(np.float32) * 0.05)(2, 512))
    _L0_wmod = _w((lambda *s: np.random.randn(*s).astype(np.float32) * 0.05)(512, 6 * 512) * 512 ** (-0.5))
    _d = {'L0_attn_x': _L0_attn_in['x'], 'L0_attn_w_qkv': _L0_attn_in['w_qkv'], 'L0_attn_w_swiglu': _L0_attn_in['w_swiglu'], 'L0_attn_w_out': _L0_attn_in['w_out'], 'L0_ffn_gate_w': _L0_ffn_in['gate_w'], 'L0_ffn_w1': _L0_ffn_in['w1'], 'L0_ffn_b1': _L0_ffn_in['b1'], 'L0_ffn_w2': _L0_ffn_in['w2'], 'L0_ffn_b2': _L0_ffn_in['b2'], 'L0_ffn_shared_w1': _L0_ffn_in['shared_w1'], 'L0_ffn_shared_b1': _L0_ffn_in['shared_b1'], 'L0_ffn_shared_w2': _L0_ffn_in['shared_w2'], 'L0_ffn_shared_b2': _L0_ffn_in['shared_b2'], 'L0_c': _L0_c, 'L0_wmod': _L0_wmod}
    _x0 = _d['L0_attn_x']
    _d['L0_attn_x'] = jax.random.normal(jax.random.fold_in(jax.random.key(seed), 1), (2, 2048, 512), dtype=_x0.dtype)
    del _x0
    return _d

def reference(L0_attn_x, L0_attn_w_qkv, L0_attn_w_swiglu, L0_attn_w_out, L0_ffn_gate_w, L0_ffn_w1, L0_ffn_b1, L0_ffn_w2, L0_ffn_b2, L0_ffn_shared_w1, L0_ffn_shared_b1, L0_ffn_shared_w2, L0_ffn_shared_b2, L0_c, L0_wmod):

    def _L0_attn_ref(x, w_qkv, w_swiglu, w_out):
        import jax, jax.numpy as jnp
        import numpy as np
        EPS = 1.1920929e-07

        def _rms(x):
            return x * jax.lax.rsqrt(jnp.mean(x * x, axis=-1, keepdims=True) + EPS)
        qkv = _rms(x) @ w_qkv.T
        q, k, v = jnp.split(qkv, 3, axis=-1)
        q = _rms(q)
        k = _rms(k)
        w = jnp.exp(k)
        kv_cum = jnp.cumsum(w * v, axis=1)
        w_cum = jnp.cumsum(w, axis=1)
        y = jax.nn.sigmoid(q) * (kv_cum / (w_cum + 1e-06))
        uv = y @ w_swiglu.T
        u, g = jnp.split(uv, 2, axis=-1)
        return x + u * jax.nn.silu(g) @ w_out.T

    def _L0_ffn_ref(x, gate_w, w1, b1, w2, b2, shared_w1, shared_b1, shared_w2, shared_b2):
        import jax, jax.numpy as jnp
        import numpy as np
        K = 2

        def gelu(v):
            return jax.nn.gelu(v, approximate=False)
        B, S, D = x.shape
        E = gate_w.shape[1]
        xf = x.reshape(-1, D)
        logits = xf @ gate_w
        top_logits, top_idx = jax.lax.top_k(logits, K)
        top_gates = jax.nn.softmax(top_logits, axis=-1)
        gates = jnp.sum(jax.nn.one_hot(top_idx, E, dtype=xf.dtype) * top_gates[..., None], axis=1)
        h = gelu(jnp.einsum('nd,edh->neh', xf, w1) + b1)
        out_e = jnp.einsum('neh,ehd->ned', h, w2) + b2
        routed = jnp.einsum('ne,ned->nd', gates, out_e)
        shared = gelu(xf @ shared_w1 + shared_b1) @ shared_w2 + shared_b2
        return (routed + shared).reshape(B, S, D)
    x = L0_attn_x
    mod = (_silu(L0_c) @ L0_wmod).reshape(L0_c.shape[0], 6, 1, -1)
    sa, ca, ga, sb, cb, gb = (mod[:, 0], mod[:, 1], mod[:, 2], mod[:, 3], mod[:, 4], mod[:, 5])
    ga = (2 * (ga >= 0) - 1) * jnp.maximum(jnp.abs(ga), 0.25)
    gb = (2 * (gb >= 0) - 1) * jnp.maximum(jnp.abs(gb), 0.25)
    h = _layernorm(x, axis=-1) * (1 + ca) + sa
    x = x + ga * _L0_attn_ref(h, L0_attn_w_qkv, L0_attn_w_swiglu, L0_attn_w_out)
    h = _layernorm(x, axis=-1) * (1 + cb) + sb
    x = x + gb * _L0_ffn_ref(h, L0_ffn_gate_w, L0_ffn_w1, L0_ffn_b1, L0_ffn_w2, L0_ffn_b2, L0_ffn_shared_w1, L0_ffn_shared_b1, L0_ffn_shared_w2, L0_ffn_shared_b2)
    return x

_drawn_inputs = setup_inputs


def setup_inputs(seed=0):
    import zlib

    import numpy as np

    out = dict(_drawn_inputs(seed))
    spreads = {}
    factors = {'L0_attn_w_qkv': 8.0,
     'L0_attn_w_swiglu': 8.0,
     'L0_attn_w_out': 8.0,
     'L0_ffn_gate_w': 170.887,
     'L0_ffn_w1': 200.0,
     'L0_ffn_b1': 200.0,
     'L0_ffn_w2': 187.852,
     'L0_ffn_b2': 200.0,
     'L0_ffn_shared_w1': 200.0,
     'L0_ffn_shared_b1': 200.0,
     'L0_ffn_shared_w2': 200.0,
     'L0_ffn_shared_b2': 200.0}
    for name, (base, spread) in spreads.items():
        noise = np.random.default_rng([zlib.crc32(name.encode()), seed]).standard_normal(out[name].shape)
        drawn = base * np.exp(spread * noise) if base else spread * noise
        out[name] = jnp.asarray(drawn.astype(out[name].dtype))
    for name, factor in factors.items():
        out[name] = (out[name] * factor).astype(out[name].dtype)
    return out
```

```python
from collections import namedtuple
from contextlib import ExitStack


import concourse.bass as bass
from concourse import mybir

F32 = mybir.dt.float32
F32R = mybir.dt.float32r
ALU = mybir.AluOpType
ACT = mybir.ActivationFunctionType
AX_X = mybir.AxisListType.X

P = 128
TT = 512
LN_EPS = 1e-05
RMS_EPS = 1.1920929e-07
EXP_LN_SET = "natural_log_exp_and_others"
SILU_SET = "silu_and_others"
GELU_SET = "gelu_and_others"
SA, CA, GA, SB, CB, GB = range(6)


def build(nc, x, c, wmod, w_qkv, w_swi, w_moe, b1, b2, gate_w, select, ident, rank, out):
    NT = x.shape[0]
    D = x.shape[2] // TT * P
    NC = D // P
    NB_SEQ = c.shape[1] // NC
    T_SEQ = NT // NB_SEQ
    E = gate_w.shape[1] // NC
    NG = 2 * E + 1
    NQKV = 3 * NC
    ROUTED = w_moe.shape[0] - NC
    SWI_W = w_swi.shape[2]
    MOE_W = w_moe.shape[2]
    QKV_W = NC * P
    CHW = NC * TT
    W_COLS = 8 * SWI_W
    NSUB = TT // P
    LAST = NT - 1
    NB_SWI = w_swi.shape[0] // 2
    NB_MOE = w_moe.shape[0] // 2
    assert NC == 4 and NB_SEQ == 2 and NB_SWI * SWI_W == W_COLS and NB_MOE * MOE_W <= W_COLS

    QKV_PIECES = w_qkv.shape[0]
    swi_col = [(j + NB_SWI // 2) % NB_SWI * SWI_W for j in range(NB_SWI)]
    moe_col = [(swi_col[0] + j * MOE_W) % W_COLS for j in range(NB_MOE)]
    pieces = [(w_qkv[i], i * SWI_W, SWI_W) for i in range(QKV_PIECES)]
    B0 = len(pieces)
    pieces += [(w_swi[j], swi_col[j], SWI_W) for j in range(NB_SWI)]
    C0 = len(pieces)
    pieces += [(w_swi[NB_SWI + j], swi_col[j], SWI_W) for j in range(NB_SWI)]
    D0 = len(pieces)
    pieces += [(w_moe[j], moe_col[j], MOE_W) for j in range(NB_MOE)]
    E0 = len(pieces)
    pieces += [(w_moe[NB_MOE + j], moe_col[j], MOE_W) for j in range(NB_MOE)]

    y_dram = nc.dram_tensor("y_scratch", (NT, P, CHW), F32, kind="Internal").ap()
    ra_dram = nc.dram_tensor("residual_a", (NT, P, CHW), F32, kind="Internal").ap()
    rb_dram = nc.dram_tensor("residual_b", (NT, P, CHW), F32, kind="Internal").ap()
    g_dram = nc.dram_tensor("gate_scratch", (NT, NG, TT), F32, kind="Internal").ap()

    ctx = ExitStack()
    with ctx:
        def sb(name, shape, dt=F32):
            return ctx.enter_context(nc.sbuf_tensor(name, shape, dt))

        def sem(name):
            return ctx.enter_context(nc.semaphore(name))

        def sems(suffix, names):
            return namedtuple("Sems", names)(*[sem(f"{n}_{suffix}") for n in names.split()])

        w_hi = sb("w_hi", [P, W_COLS], F32R)
        w_lo = sb("w_lo", [P, W_COLS], F32R)
        raw = [sb(f"raw{i}", [P, SWI_W]) for i in range(2)]
        x_t = sb("x_t", [P, CHW])
        r_t = sb("r_t", [P, CHW])
        sq_t = sb("sq_t", [P, CHW])
        sum_x = sb("sum_x", [P, TT])
        sum_qk = sb("sum_qk", [P, TT])
        rs_x = sb("rs_x", [P, TT])
        nt_x = sb("nt_x", [P, TT])
        rs_qk = sb("rs_qk", [P, TT])
        nt_qk = sb("nt_qk", [P, TT])
        x_hi = sb("x_hi", [P, CHW], F32R)
        x_lo = sb("x_lo", [P, CHW], F32R)
        mod_t = sb("mod_t", [P, NT, 6 * NC + 1])
        mod_raw = sb("mod_raw", [P, 6 * NC * NB_SEQ])
        mod_tmp = sb("mod_tmp", [P, 2 * NC * NB_SEQ])
        c_t = sb("c_t", [P, NC * NB_SEQ])
        c_e = sb("c_e", [P, NC * NB_SEQ])
        mean_w = sb("mean_w", [P, P])
        ident_t = sb("ident_t", [P, P])
        b1_t = sb("b1_t", [P, w_moe.shape[0]])
        gw_t = sb("gw_t", [P, NC * E])
        rank_t = sb("rank_t", [P, E])
        carry_kv = sb("carry_kv", [P, NC])
        carry_w = sb("carry_w", [P, NC])
        eps_t = sb("eps_t", [P, 2])
        eps_ln, eps_rms = eps_t[:, 0:1], eps_t[:, 1:2]

        with ExitStack() as only_a:
            def sa_(name):
                return only_a.enter_context(nc.sbuf_tensor(name, [P, CHW], F32))
            k_t, q_t, wv_t, kv_t, wc_t = [sa_(n) for n in ("k_t", "q_t", "wv_t", "kv_t", "wc_t")]
        act_t = sb("act_t", [P, 2, TT])
        s_t = sb("s_t", [P, 2, TT])
        s_hi = sb("s_hi", [P, 3, TT], F32R)
        s_lo = sb("s_lo", [P, 3, TT], F32R)
        g_next = sb("g_next", [NG, TT])
        g_rows = sb("g_rows", [NG, TT], F32R)
        sel_raw = sb("sel_raw", [2 * E, E * P])
        sel_t = sb("sel_t", [2 * E, E * P], F32R)
        b2_raw = sb("b2_raw", [NG, D])
        b2_hi = sb("b2_hi", [NG, D], F32R)
        b2_lo = sb("b2_lo", [NG, D], F32R)
        gates_tok = sb("gates_tok", [P, NSUB, P])
        lg = sb("lg", [P, NSUB, E])
        eq = sb("eq", [P, NSUB, E])
        top1 = sb("top1", [P, NSUB, E])
        lg2 = sb("lg2", [P, NSUB, E])
        top2 = sb("top2", [P, NSUB, E])
        m1 = sb("m1", [P, NSUB])
        m2 = sb("m2", [P, NSUB])
        fst = sb("fst", [P, NSUB])
        g1 = sb("g1", [P, NSUB])
        g2 = sb("g2", [P, NSUB])
        bank = [ctx.enter_context(nc.psum_tensor(f"bank{i}", [P, TT], F32)) for i in range(8)]
        b_qk, b_x = bank[6], bank[7]

        const_in, c_in, wmod_in, sel_in = sem("const_in"), sem("c_in"), sem("wmod_in"), sem("sel_in")
        raw_in = [sem("raw_in0"), sem("raw_in1")]
        w_hi_ok, w_ok = sem("w_hi_ok"), sem("w_ok")
        ones_ok, carry_ok, keep_ok = sem("ones_ok"), sem("carry_ok"), sem("keep_ok")
        c_exp, c_silu, mod_mm, mod_cp, mod_ok = [sem(n) for n in ("c_exp", "c_silu", "mod_mm", "mod_cp", "mod_ok")]
        x_in, r_in, r_st = sem("x_in"), sem("r_in"), sem("r_st")
        xh_ok, xl_ok = sem("xh_ok"), sem("xl_ok")
        y_st, h_st, g_st, out_st = sem("y_st"), sem("h_st"), sem("g_st"), sem("out_st")
        g_in = sem("g_in")
        sel_ok = sem("sel_ok")
        settled = sem("settled")
        setup_v = sem("setup_v")
        LN = ("sum0 mean_mm d_ok dsq_ok sum1 var_mm ln_ok seed_ok newton rstd_ok dr_ok h_ok half")
        na = sems("norm_a", LN + " hsq_ok sum2 rms_mm lnr_ok seedr_ok rrms_ok n_ok r_ok")
        nd = sems("norm_d", LN + " logit_mm top_ok e_ok gate_chain gt_ok tr_mm gp_ok")
        a = sems("qkv", "mm kq_ev ksum k_mm ln_k seed_k newton rk_ok kn_ok w_ok qsum q_mm ln_q seed_q rq_ok qn_ok "
                      "e_ok wv_ok scan_ok carry denp den_ok rcp_ok y_ok halfqk")
        ffn = {p: sems(p, "up act_ok s_ok sh_ok sl_ok dn ev_ok gb") for p in "bcde"}
        g_cp, gate_fin = sem("g_cp"), sem("gate_fin")

        PASS = {"a": 0, "b": 1, "c": 2, "d": 3, "e": 4}
        NB = {"b": NB_SWI, "c": NB_SWI, "d": NB_MOE, "e": NB_MOE}
        W0 = {"b": B0, "c": C0, "d": D0, "e": E0}
        UPS = {"b": 2, "c": 2, "d": 1, "e": 1}
        GAIN = {"b": GA, "c": GA, "d": GB, "e": GB}
        NEXT = {"a": "b", "b": "c", "c": "d", "d": "e"}
        N_ROUTED = {"b": 0, "c": 0, "d": NB_MOE, "e": ROUTED - NB_MOE}
        HOOKS_C = dict(mean=1, sq=2, var=3, h=4, logit=5, e=6, tr=7)
        HOOKS_D = dict(mean=2, sq=3, var=4, h=6, logit=7, e=8, tr=9)

        def ch(t, m):
            return t[:, m * TT:(m + 1) * TT]

        def rows(t):
            return t[:, :].rearrange("p (c n) -> p c n", c=NC)

        def over_chunks(t):
            return t[:, :].rearrange("p (o n) -> p o n", o=1).broadcast_to([P, NC, TT])

        def vec(t, v, m):
            return mod_t[:, t, v * NC + m:v * NC + m + 1]

        block = ctx.enter_context(nc.Block())

        @block.sync
        def _(sp):
            def piece(i):
                if i >= 2:
                    sp.wait_ge(w_ok, i - 1)
                src, _, n = pieces[i]
                sp.dma_start(raw[i % 2][:, 0:n], src).then_inc(raw_in[i % 2], 16)

            def load_x(src, t):
                sp.dma_start(x_t[:, :], src[t]).then_inc(x_in, 16)

            def load_r(src, t):
                sp.dma_start(r_t[:, :], src[t]).then_inc(r_in, 16)

            sp.dma_start(c_t[:, :], c).then_inc(c_in, 16)
            load_x(x, 0)
            wmod_bufs = [k_t, q_t, wv_t, kv_t, wc_t, r_t]
            for v in range(6):
                sp.dma_start(wmod_bufs[v][:, :], wmod[v]).then_inc(wmod_in, 16)
                if v == 1:
                    piece(0)
                    piece(1)
            sp.dma_start(ident_t[:, :], ident).then_inc(const_in, 16)
            sp.dma_start(b1_t[:, :], b1).then_inc(const_in, 16)
            sp.dma_start(gw_t[:, :], gate_w).then_inc(const_in, 16)
            sp.dma_start(rank_t[:, :], rank).then_inc(const_in, 16)
            sp.wait_ge(mod_mm, 1)
            load_r(x, 0)
            for i in range(2, B0 + NB_SWI // 2 + 2):
                piece(i)
            sp.wait_ge(na.r_ok, NC)
            sp.dma_start(ra_dram[0], r_t[:, :]).then_inc(r_st, 16)

            def tile_a(t, first=False, last=False):
                u = t + 1
                sp.wait_ge(xl_ok, NC * u)
                if not last:
                    load_x(x, u)
                    sp.wait_ge(r_st, 16 * u)
                    sp.sem_inc(settled)
                    load_r(x, u)
                else:
                    sp.wait_ge(y_st, 16)
                    load_x(y_dram, 0)
                if not first:
                    sp.wait_ge(a.y_ok, NC * t)
                    sp.sem_inc(settled)
                    sp.dma_start(y_dram[t - 1], kv_t[:, :]).then_inc(y_st, 16)
                if not last:
                    sp.wait_ge(na.r_ok, NC * (u + 1))
                    sp.sem_inc(settled)
                    sp.dma_start(ra_dram[u], r_t[:, :]).then_inc(r_st, 16)

            tile_a(0, first=True)
            with sp.Fori(1, LAST) as t:
                tile_a(t)
            tile_a(LAST, last=True)
            sp.wait_ge(a.y_ok, NC * NT)
            sp.dma_start(y_dram[LAST], kv_t[:, :]).then_inc(y_st, 16)
            sp.wait_ge(y_st, 16 * NT)
            sp.dma_start(sel_raw[:, :], select).then_inc(sel_in, 16)
            sp.dma_start(b2_raw[:, :], b2).then_inc(sel_in, 16)
            sp.wait_ge(r_st, 16 * NT)
            sp.dma_start(r_t[:, :], ra_dram[0]).then_inc(r_in, 16)
            for i in range(B0 + NB_SWI // 2 + 2, C0):
                piece(i)

            X_SRC = {"b": y_dram, "c": y_dram, "d": ra_dram, "e": y_dram}
            R_SRC = {"b": ra_dram, "c": rb_dram, "d": ra_dram, "e": rb_dram}
            R_DST = {"b": rb_dram, "c": ra_dram, "d": rb_dram, "e": out}

            def next_x(p, t):
                sp.wait_ge(xl_ok, NC * (NT * PASS[p] + t))
                if p == "b":
                    sp.sem_inc(settled)
                    sp.wait_ge(y_st, 16 * (t + 1))
                if p == "d":
                    sp.sem_inc(settled)
                    sp.wait_ge(r_st, 16 * (2 * NT + t + 1))
                    sp.sem_inc(settled)
                    sp.wait_ge(h_st, 16 * t)
                if p == "e":
                    sp.sem_inc(settled)
                    sp.wait_ge(h_st, 16 * NT)
                    sp.wait_ge(g_cp, NT + t)
                    sp.sem_inc(settled)
                    sp.wait_ge(g_st, 16 * NT)
                sp.sem_inc(settled)
                load_x(X_SRC[p], t)
                if p == "e":
                    sp.dma_start(g_next[:, :], g_dram[t]).then_inc(g_in, 16)

            def store_h(t):
                sp.wait_ge(nd.h_ok, NC * (t + 1))
                sp.sem_inc(settled)
                sp.dma_start(y_dram[t], x_t[:, :]).then_inc(h_st, 16)
                sp.wait_ge(nd.gp_ok, t + 1)
                sp.sem_inc(settled)
                sp.dma_start(g_dram[t], g_next[:, :]).then_inc(g_st, 16)

            def tile(p, t, last=False):
                if not last:
                    next_x(p, t + 1)
                elif p != "e":
                    next_x(NEXT[p], 0)
                if last and p != "e":
                    n0 = W0[NEXT[p]]
                    for i in range(n0, n0 + NB[NEXT[p]]):
                        piece(i)
                if p == "d" and not last:
                    store_h(t + 1)
                if p == "c" and last:
                    store_h(0)
                sp.wait_ge(ffn[p].ev_ok, NC * (t + 1))
                sp.sem_inc(settled)
                if p == "e":
                    sp.dma_start(R_DST[p][t], r_t[:, :]).then_inc(out_st, 16)
                    sp.wait_ge(out_st, 16 * (t + 1))
                else:
                    sp.dma_start(R_DST[p][t], r_t[:, :]).then_inc(r_st, 16)
                    sp.wait_ge(r_st, 16 * (NT * PASS[p] + t + 1))
                sp.sem_inc(settled)
                if not last:
                    load_r(R_SRC[p], t + 1)
                elif p != "e":
                    load_r(R_SRC[NEXT[p]], 0)

            for p in "bcde":
                with sp.Fori(0, LAST) as t:
                    tile(p, t)
                tile(p, LAST, last=True)
            for s, n in ((y_st, 16 * NT), (h_st, 16 * NT), (g_st, 16 * NT), (r_st, 4 * 16 * NT), (out_st, 16 * NT)):
                sp.wait_ge(s, n)

        @block.gpsimd
        def _(pool):
            def piece(i):
                _, col, n = pieces[i]
                pool.wait_ge(raw_in[i % 2], 16 * (i // 2 + 1))
                src = raw[i % 2][:, 0:n]
                nc.gpsimd.tensor_scalar(w_hi[:, col:col + n], src, 1.0, 1.0, ALU.mult, ALU.mult).then_inc(w_hi_ok, 1)
                pool.wait_ge(w_hi_ok, i + 1)
                nc.gpsimd.tensor_tensor(w_lo[:, col:col + n], src, w_hi[:, col:col + n].bitcast(F32),
                                        ALU.subtract).then_inc(w_ok, 1)

            def chunk_sum(dst, src, pair, half_done, n, done):
                nc.gpsimd.tensor_tensor(pair[:, 0:2 * TT], src[:, 0:CHW // 2], src[:, CHW // 2:CHW],
                                        ALU.add).then_inc(half_done, 1)
                pool.wait_ge(half_done, n + 1)
                nc.gpsimd.tensor_tensor(dst[:, :], pair[:, 0:TT], pair[:, TT:2 * TT],
                                        ALU.add).then_inc(done, 1)

            def sum_x0(n, u, xs, per):
                pool.wait_ge(x_in, 16 * (xs + u + 1))
                chunk_sum(sum_x, x_t, sq_t, n.half, per * u, n.sum0)

            def sum_d(n, u, per):
                pool.wait_ge(n.dsq_ok, u + 1)
                chunk_sum(sum_x, sq_t, sq_t, n.half, per * u + 1, n.sum1)

            def sum_h(u):
                pool.wait_ge(na.hsq_ok, u + 1)
                chunk_sum(sum_x, sq_t, sq_t, na.half, 3 * u + 2, na.sum2)

            for i in range(2):
                piece(i)
            sum_x0(na, 0, 0, 3)
            piece(2)
            sum_d(na, 0, 3)
            piece(3)
            sum_h(0)
            for i in range(4, B0 + NB_SWI // 2):
                piece(i)

            def tile_a(t, last=False):
                u = t + 1
                if not last:
                    pool.wait_ge(na.rms_mm, u)
                    sum_x0(na, u, 0, 3)
                pool.wait_ge(a.kq_ev, 2 * NC * t + NC)
                chunk_sum(sum_qk, wv_t, wv_t, a.halfqk, 2 * t, a.ksum)
                if not last:
                    sum_d(na, u, 3)
                pool.wait_ge(a.rk_ok, t + 1)
                nc.gpsimd.tensor_tensor(rows(k_t), rows(k_t), over_chunks(rs_qk), ALU.mult).then_inc(a.kn_ok, 1)
                pool.wait_ge(a.kq_ev, 2 * NC * (t + 1))
                chunk_sum(sum_qk, wv_t, wv_t, a.halfqk, 2 * t + 1, a.qsum)
                if not last:
                    sum_h(u)
                pool.wait_ge(a.rq_ok, t + 1)
                nc.gpsimd.tensor_tensor(rows(q_t), rows(q_t), over_chunks(rs_qk), ALU.mult).then_inc(a.qn_ok, 1)

            with pool.Fori(0, LAST) as t:
                tile_a(t)
            tile_a(LAST, last=True)
            pool.wait_ge(a.mm, NQKV * NT)
            for i in range(B0 + NB_SWI // 2, C0):
                piece(i)
            pool.wait_ge(sel_in, 32)
            nc.gpsimd.tensor_scalar(sel_t[:, :], sel_raw[:, :], 1.0, None, ALU.mult).then_inc(sel_ok, 1)
            nc.gpsimd.tensor_scalar(b2_hi[:, :], b2_raw[:, :], 1.0, None, ALU.mult).then_inc(sel_ok, 1)
            pool.wait_ge(sel_ok, 2)
            nc.gpsimd.tensor_tensor(b2_lo[:, :], b2_raw[:, :], b2_hi[:, :].bitcast(F32),
                                    ALU.subtract).then_inc(sel_ok, 1)

            def freed_by(col, n, cols, width):
                return max(j for j, k in enumerate(cols) if k < col + n and col < k + width)

            for j in range(NB_SWI):
                pool.wait_ge(ffn["b"].dn, NB_SWI * LAST + j + 1)
                piece(C0 + j)
            for j in range(NB_MOE):
                if j == 0:
                    sum_x0(nd, 0, 3 * NT, 2)
                if j == 1:
                    sum_d(nd, 0, 2)
                pool.wait_ge(ffn["c"].dn, NB_SWI * LAST + freed_by(moe_col[j], MOE_W, swi_col, SWI_W) + 1)
                piece(D0 + j)
            with pool.Fori(0, LAST) as t:
                pool.wait_ge(nd.var_mm, t + 1)
                sum_x0(nd, t + 1, 3 * NT, 2)
                sum_d(nd, t + 1, 2)
            for j in range(NB_MOE):
                pool.wait_ge(ffn["d"].dn, NB_MOE * LAST + j + 1)
                piece(E0 + j)

        @block.tensor
        def _(pe):
            def product(dst, rhs_hi, rhs_lo, col, start, stop):
                nc.tensor.matmul(dst, w_hi[:, col:col + P], rhs_hi, start=start, stop=False)
                nc.tensor.matmul(dst, w_hi[:, col:col + P], rhs_lo, start=False, stop=False)
                return nc.tensor.matmul(dst, w_lo[:, col:col + P], rhs_hi, start=False, stop=stop)

            def from_x(dst, col, first_of_tile=None):
                for m in range(NC):
                    if first_of_tile is not None:
                        pe.wait_ge(xl_ok, first_of_tile + m + 1)
                    ins = product(dst, ch(x_hi, m), ch(x_lo, m), col + m * P, m == 0, m == NC - 1)
                return ins

            def mean(dst, src):
                return nc.tensor.matmul(dst[:, :], mean_w[:, :], src[:, :], start=True, stop=True)

            pe.wait_ge(ones_ok, 1)
            pe.wait_ge(wmod_in, 6 * 16)
            pe.wait_ge(c_silu, 1)
            wmod_bufs = [k_t, q_t, wv_t, kv_t, wc_t, r_t]
            for v in range(6):
                for m in range(NC):
                    at = (v * NC + m) * NB_SEQ
                    for k in range(NC):
                        ins = nc.tensor.matmul(b_qk[:, at:at + NB_SEQ],
                                               wmod_bufs[v][:, k * D + m * P:k * D + (m + 1) * P],
                                               c_t[:, k * NB_SEQ:(k + 1) * NB_SEQ], start=(k == 0), stop=(k == NC - 1))
            ins.then_inc(mod_mm, 1)

            def norm_mean(n, u):
                pe.wait_ge(n.sum0, u + 1)
                mean(b_x, sum_x).then_inc(n.mean_mm, 1)

            def norm_var(n, u):
                pe.wait_ge(n.sum1, u + 1)
                mean(b_x, sum_x).then_inc(n.var_mm, 1)

            def norm_rms(u):
                pe.wait_ge(na.sum2, u + 1)
                mean(b_x, sum_x).then_inc(na.rms_mm, 1)

            norm_mean(na, 0)
            norm_var(na, 0)
            norm_rms(0)

            def tile_a(t, last=False):
                u = t + 1
                for o in range(NQKV):
                    pe.wait_ge(w_ok, o // 3 + 1)
                    if o >= 6:
                        pe.wait_ge(a.kq_ev, 2 * NC * t + o - 5)
                    from_x(bank[o % 6][:, :], o * QKV_W, NC * t if o == 0 else None).then_inc(a.mm, 1)
                    if o == 3 and not last:
                        norm_mean(na, u)
                    if o == 5:
                        pe.wait_ge(a.ksum, t + 1)
                        mean(b_qk, sum_qk).then_inc(a.k_mm, 1)
                    if o == 7 and not last:
                        norm_var(na, u)
                    if o == 8:
                        pe.wait_ge(a.qsum, t + 1)
                        mean(b_qk, sum_qk).then_inc(a.q_mm, 1)
                    if o == 10 and not last:
                        norm_rms(u)

            pe.wait_ge(mod_cp, 1)
            with pe.Fori(0, LAST) as t:
                tile_a(t)
            tile_a(LAST, last=True)

            def logits(u):
                pe.wait_ge(nd.h_ok, NC * (u + 1))
                for s in range(NSUB):
                    for m in range(NC):
                        ins = nc.tensor.matmul(b_x[:, s * E:(s + 1) * E],
                                               x_t[:, m * TT + s * P:m * TT + (s + 1) * P],
                                               gw_t[:, m * E:(m + 1) * E], start=(m == 0), stop=(m == NC - 1))
                ins.then_inc(nd.logit_mm, 1)

            def gates_to_rows(u):
                pe.wait_ge(nd.gt_ok, u + 1)
                for s in range(NSUB):
                    ins = nc.tensor.transpose(b_x[:, s * P:(s + 1) * P], gates_tok[:, s, :], ident_t[:, :])
                ins.then_inc(nd.tr_mm, 1)

            def hooks(h, s, u):
                if s == h["mean"]:
                    norm_mean(nd, u)
                if s == h["var"]:
                    norm_var(nd, u)
                if s == h["logit"]:
                    logits(u)
                if s == h["tr"]:
                    gates_to_rows(u)

            def up(p, t, s):
                f, nb = ffn[p], NB[p]
                pe.wait_ge(w_ok, W0[p] + s + 1)
                first = NC * (NT * PASS[p] + t) if s == 0 else None
                if UPS[p] == 2:
                    for half in range(2):
                        o = 2 * s + half
                        if o >= 3:
                            read = f.s_ok if (o - 3) % 2 else f.act_ok
                            pe.wait_ge(read, nb * t + (o - 3) // 2 + 1)
                        from_x(bank[4 + o % 3][:, :], swi_col[s] + half * QKV_W,
                               first if half == 0 else None).then_inc(f.up, 1)
                    return
                if s % 2 == 0 and s < N_ROUTED[p]:
                    e = (0 if p == "d" else NB_MOE // 2) + s // 2
                    if s == 0:
                        pe.wait_ge(g_cp, (NT if p == "e" else 0) + t + 1)
                        pe.wait_ge(sel_ok, 3)
                    if s > 0:
                        pe.wait_ge(f.s_ok, nb * t + s)
                    nc.tensor.matmul(bank[6][:, :], sel_t[:, e * P:(e + 1) * P], g_rows[0:2 * E, :],
                                     start=True, stop=True).then_inc(f.gb, 1)
                if s >= 2:
                    pe.wait_ge(f.act_ok, nb * t + s - 1)
                from_x(bank[4 + s % 2][:, :], moe_col[s], first).then_inc(f.up, 1)

            def down(p, t, s):
                f, nb = ffn[p], NB[p]
                pe.wait_ge(f.sl_ok, nb * t + s + 1)
                if s == 0:
                    if p == "e":
                        for m in range(NC):
                            for part in (b2_hi, b2_lo):
                                ins = nc.tensor.matmul(bank[m][:, :], part[:, m * P:(m + 1) * P], g_rows[:, :],
                                                       start=part is b2_hi, stop=False)
                        ins.then_inc(f.gb, 1)
                col = swi_col[s] + 2 * QKV_W if UPS[p] == 2 else moe_col[s] + QKV_W
                for m in range(NC):
                    ins = product(bank[m][:, :], s_hi[:, s % 3, :], s_lo[:, s % 3, :], col + m * P,
                                  s == 0 and p != "e", s == nb - 1)
                ins.then_inc(f.dn, 1)

            def tile(p, t, last=False):
                for s in range(NB[p] + 2):
                    if s < NB[p]:
                        up(p, t, s)
                    if s >= 2:
                        down(p, t, s - 2)
                    if p == "d" and not last:
                        hooks(HOOKS_D, s, t + 1)
                    if p == "c" and last:
                        hooks(HOOKS_C, s, 0)

            pe.wait_ge(const_in, 4 * 16)
            for p in "bcde":
                if p == "b":
                    pe.wait_ge(a.wv_ok, NC * NT)
                    pe.wait_ge(a.kq_ev, 2 * NC * NT)
                    pe.wait_ge(a.rq_ok, NT)
                else:
                    prev = ffn[{"c": "b", "d": "c", "e": "d"}[p]]
                    nbp = NB[{"c": "b", "d": "c", "e": "d"}[p]]
                    pe.wait_ge(prev.s_ok, nbp * NT)
                with pe.Fori(0, LAST) as t:
                    tile(p, t)
                tile(p, LAST, last=True)

        @block.scalar
        def _(act):
            act.wait_ge(c_in, 16)
            nc.scalar.preload_act_table_set(EXP_LN_SET)
            nc.scalar.activation(c_e[:, :], c_t[:, :], ACT.Exp, scale=-1.0).then_inc(c_exp, 1)

            def rsqrt_seed(dst, src, eps, ln_done, n, seed_done):
                nc.scalar.activation(dst[:, :], src[:, :], ACT.Ln, bias=eps).then_inc(ln_done, 1)
                act.wait_ge(ln_done, n + 1)
                nc.scalar.activation(dst[:, :], dst[:, :], ACT.Exp, scale=-0.5).then_inc(seed_done, 1)

            def split(g, ready, count):
                act.wait_ge(ready, count)
                for m in range(NC):
                    nc.scalar.activation(ch(x_hi, m), ch(x_t, m), ACT.Copy).then_inc(xh_ok, 1)

            def norm_sq(n, u):
                act.wait_ge(n.d_ok, u + 1)
                nc.scalar.activation(sq_t[:, :], x_t[:, :], ACT.Square).then_inc(n.dsq_ok, 1)

            def norm_seed(n, u):
                act.wait_ge(n.var_mm, u + 1)
                rsqrt_seed(rs_x, b_x, eps_ln, n.ln_ok, u, n.seed_ok)

            def norm_h(n, u, c_vec, s_vec):
                act.wait_ge(n.dr_ok, u + 1)
                for m in range(NC):
                    nc.scalar.activation(ch(x_t, m), ch(x_t, m), ACT.Identity, bias=vec(u, s_vec, m),
                                         scale=vec(u, c_vec, m)).then_inc(n.h_ok, 1)

            def norm_hsq(u):
                act.wait_ge(na.h_ok, NC * (u + 1))
                act.wait_ge(na.sum1, u + 1)
                nc.scalar.activation(sq_t[:, :], x_t[:, :], ACT.Square).then_inc(na.hsq_ok, 1)

            def norm_rseed(u):
                act.wait_ge(na.rms_mm, u + 1)
                rsqrt_seed(rs_x, b_x, eps_rms, na.lnr_ok, u, na.seedr_ok)

            def square_out(m, o, dst, t):
                act.wait_ge(a.mm, NQKV * t + o + 1)
                nc.scalar.activation(ch(dst, m), bank[o % 6][:, :], ACT.Copy)
                nc.scalar.activation(ch(wv_t, m), bank[o % 6][:, :], ACT.Square).then_inc(a.kq_ev, 1)

            act.wait_ge(mod_ok, 1)
            act.wait_ge(const_in, 4 * 16)
            norm_sq(na, 0)
            norm_seed(na, 0)
            norm_h(na, 0, CA, SA)
            norm_hsq(0)
            norm_rseed(0)
            split(0, na.n_ok, 1)

            def tile_a(t, last=False):
                u = t + 1
                for m in range(NC):
                    square_out(m, m, k_t, t)
                if not last:
                    act.wait_ge(na.sum2, u)
                    norm_sq(na, u)
                act.wait_ge(a.k_mm, t + 1)
                rsqrt_seed(rs_qk, b_qk, eps_rms, a.ln_k, t, a.seed_k)
                act.wait_ge(a.ksum, t + 1)
                for m in range(NC // 2):
                    square_out(m, NC + m, q_t, t)
                if not last:
                    norm_seed(na, u)
                for m in range(NC // 2, NC):
                    square_out(m, NC + m, q_t, t)
                act.wait_ge(a.kn_ok, t + 1)
                nc.scalar.activation(k_t[:, :], k_t[:, :], ACT.Exp).then_inc(a.w_ok, 1)
                if not last:
                    norm_h(na, u, CA, SA)
                    norm_hsq(u)
                act.wait_ge(a.q_mm, t + 1)
                rsqrt_seed(rs_qk, b_qk, eps_rms, a.ln_q, t, a.seed_q)
                if not last:
                    norm_rseed(u)
                act.wait_ge(a.qn_ok, t + 1)
                nc.scalar.activation(q_t[:, :], q_t[:, :], ACT.Exp, scale=-1.0).then_inc(a.e_ok, 1)
                act.wait_ge(a.mm, NQKV * (t + 1))
                if not last:
                    split(u, na.n_ok, u + 1)
                else:
                    split(NT, x_in, 16 * (NT + 1))

            with act.Fori(0, LAST) as t:
                tile_a(t)
            tile_a(LAST, last=True)
            act.wait_ge(a.den_ok, NT)

            def hooks(h, s, u, back_to):
                if s == h["sq"]:
                    norm_sq(nd, u)
                if s == h["var"]:
                    nc.scalar.preload_act_table_set(EXP_LN_SET)
                    norm_seed(nd, u)
                if s == h["h"]:
                    norm_h(nd, u, CB, SB)
                if s == h["e"]:
                    nc.scalar.preload_act_table_set(EXP_LN_SET)
                    act.wait_ge(nd.top_ok, u + 1)
                    nc.scalar.activation(g2[:, :], m2[:, :], ACT.Exp).then_inc(nd.e_ok, 1)
                if s in (h["var"], h["e"]):
                    nc.scalar.preload_act_table_set(back_to)

            def take_gates(u, first):
                act.wait_ge(nd.tr_mm, u + 1)
                if not first:
                    act.wait_ge(g_st, 16 * u)
                nc.scalar.activation(g_next[:, :], b_x[0:NG, :], ACT.Copy).then_inc(nd.gp_ok, 1)

            def block_(p, t, s):
                f, nb = ffn[p], NB[p]
                act.wait_ge(f.up, UPS[p] * (nb * t + s) + 1)
                if UPS[p] == 2:
                    nc.scalar.activation(act_t[:, s % 2, :], bank[4 + 2 * s % 3][:, :], ACT.Silu).then_inc(f.act_ok, 1)
                else:
                    j = s + (NB_MOE if p == "e" else 0)
                    nc.scalar.activation(act_t[:, s % 2, :], bank[4 + s % 2][:, :], ACT.Gelu,
                                         bias=b1_t[:, j:j + 1]).then_inc(f.act_ok, 1)
                act.wait_ge(f.s_ok, nb * t + s + 1)
                nc.scalar.activation(s_hi[:, s % 3, :], s_t[:, s % 2, :], ACT.Copy).then_inc(f.sh_ok, 1)

            def rows_of_gates(p, t):
                if p == "d":
                    act.wait_ge(nd.gp_ok, t + 1)
                else:
                    act.wait_ge(g_in, 16 * (t + 1))
                nc.scalar.activation(g_rows[:, :], g_next[:, :], ACT.Copy).then_inc(g_cp, 1)

            def tile(p, t, last=False):
                f = ffn[p]
                for s in range(NB[p]):
                    block_(p, t, s)
                    if p == "d" and not last:
                        hooks(HOOKS_D, s, t + 1, GELU_SET)
                    if p == "c" and last:
                        hooks(HOOKS_C, s, 0, SILU_SET)
                if last and p == "e":
                    return
                q, u = (NEXT[p], 0) if last else (p, t + 1)
                act.wait_ge(f.up, UPS[p] * NB[p] * (t + 1))
                g = NT * PASS[q] + u
                if q == "d":
                    split(g, nd.h_ok, NC * (u + 1))
                    take_gates(u, last)
                else:
                    split(g, x_in, 16 * (g + 1))
                if q in "de":
                    rows_of_gates(q, u)

            for p in "bcde":
                nc.scalar.preload_act_table_set(SILU_SET if UPS[p] == 2 else GELU_SET)
                with act.Fori(0, LAST) as t:
                    tile(p, t)
                tile(p, LAST, last=True)

        @block.vector
        def _(dve):
            nc.vector.memset(eps_ln, LN_EPS)
            nc.vector.memset(eps_rms, RMS_EPS)
            nc.vector.memset(mean_w[:, :], 1.0 / D).then_inc(ones_ok, 1)
            nc.vector.memset(carry_kv[:, :], 0.0).then_inc(carry_ok, 1)
            nc.vector.memset(carry_w[:, :], 0.0).then_inc(carry_ok, 1)
            nc.vector.memset(mod_t[:, :, 6 * NC:6 * NC + 1], 1.0).then_inc(keep_ok, 1)
            dve.wait_ge(c_exp, 1)
            nc.vector.tensor_scalar(c_e[:, :], c_e[:, :], 1.0, None, ALU.add).then_inc(setup_v, 1)
            dve.wait_ge(setup_v, 1)
            nc.vector.reciprocal(c_e[:, :], c_e[:, :]).then_inc(setup_v, 1)
            dve.wait_ge(setup_v, 2)
            nc.vector.tensor_tensor(c_t[:, :], c_t[:, :], c_e[:, :], ALU.mult).then_inc(c_silu, 1)
            dve.wait_ge(keep_ok, 1)
            nc.vector.memset(mod_t[:, T_SEQ - 1, 6 * NC:6 * NC + 1], 0.0)
            dve.wait_ge(mod_mm, 1)
            nc.vector.tensor_copy(mod_raw[:, :], b_qk[:, 0:6 * NC * NB_SEQ]).then_inc(mod_cp, 1)
            dve.wait_ge(mod_cp, 1)
            mods = mod_raw[:, :].rearrange("p (v n) -> p v n", v=6)
            tmp = mod_tmp[:, :].rearrange("p (v n) -> p v n", v=2)
            scales, gains = mods[:, CA:CB + 1:3, :], mods[:, GA:GB + 1:3, :]
            nc.vector.tensor_scalar(scales, scales, 1.0, None, ALU.add).then_inc(setup_v, 1)
            nc.vector.tensor_scalar(tmp, gains, 0.0, 2.0, ALU.is_ge, ALU.mult).then_inc(setup_v, 1)
            dve.wait_ge(setup_v, 4)
            nc.vector.tensor_scalar(tmp, tmp, 1.0, None, ALU.subtract).then_inc(setup_v, 1)
            dve.wait_ge(setup_v, 5)
            nc.vector.tensor_tensor(gains, gains, tmp, ALU.mult).then_inc(setup_v, 1)
            dve.wait_ge(setup_v, 6)
            nc.vector.scalar_tensor_tensor(out=gains, in0=gains, scalar=0.25, in1=tmp, op0=ALU.max,
                                           op1=ALU.mult).then_inc(setup_v, 1)
            dve.wait_ge(setup_v, 7)
            by_seq = mod_raw[:, :].rearrange("p (k b o) -> p b o k", b=NB_SEQ, o=1)
            for b in range(NB_SEQ):
                ins = nc.vector.tensor_copy(mod_t[:, b * T_SEQ:(b + 1) * T_SEQ, 0:6 * NC],
                                            by_seq[:, b].broadcast_to([P, T_SEQ, 6 * NC]))
            ins.then_inc(mod_ok, 1)

            def newton(y, f, src, eps, chain, n, done):
                nc.vector.tensor_tensor(f[:, :], y[:, :], y[:, :], ALU.mult).then_inc(chain, 1)
                dve.wait_ge(chain, n + 1)
                nc.vector.scalar_tensor_tensor(out=f[:, :], in0=src[:, :], scalar=eps, in1=f[:, :],
                                               op0=ALU.add, op1=ALU.mult).then_inc(chain, 1)
                dve.wait_ge(chain, n + 2)
                dve.sem_inc(settled)
                nc.vector.tensor_scalar(f[:, :], f[:, :], -0.5, 1.5, ALU.mult, ALU.add).then_inc(chain, 1)
                dve.wait_ge(chain, n + 3)
                dve.sem_inc(settled)
                nc.vector.tensor_tensor(y[:, :], y[:, :], f[:, :], ALU.mult).then_inc(done, 1)

            def split(g):
                for m in range(NC):
                    dve.wait_ge(xh_ok, g + m + 1)
                    dve.sem_inc(settled)
                    nc.vector.tensor_tensor(ch(x_lo, m), ch(x_t, m), ch(x_hi, m).bitcast(F32),
                                            ALU.subtract).then_inc(xl_ok, 1)

            def norm_d(n, u):
                dve.wait_ge(n.mean_mm, u + 1)
                dve.sem_inc(settled)
                nc.vector.tensor_tensor(rows(x_t), rows(x_t), over_chunks(b_x), ALU.subtract).then_inc(n.d_ok, 1)

            def times_rs(done):
                nc.vector.tensor_tensor(rows(x_t), rows(x_t), over_chunks(rs_x), ALU.mult).then_inc(done, 1)

            def norm_rstd(n, u, per):
                dve.wait_ge(n.seed_ok, u + 1)
                dve.sem_inc(settled)
                newton(rs_x, nt_x, b_x, LN_EPS, n.newton, per * u, n.rstd_ok)
                dve.wait_ge(n.rstd_ok, u + 1)
                dve.sem_inc(settled)
                times_rs(n.dr_ok)

            def norm_rest(u):
                dve.wait_ge(r_in, 16 * (u + 1))
                dve.sem_inc(settled)
                for m in range(NC):
                    dve.wait_ge(na.h_ok, NC * u + m + 1)
                    dve.sem_inc(settled)
                    nc.vector.scalar_tensor_tensor(out=ch(r_t, m), in0=ch(x_t, m), scalar=vec(u, GA, m),
                                                   in1=ch(r_t, m), op0=ALU.mult, op1=ALU.add).then_inc(na.r_ok, 1)
                dve.wait_ge(na.seedr_ok, u + 1)
                dve.sem_inc(settled)
                newton(rs_x, nt_x, b_x, RMS_EPS, na.newton, 6 * u + 3, na.rrms_ok)
                dve.wait_ge(na.rrms_ok, u + 1)
                dve.sem_inc(settled)
                times_rs(na.n_ok)

            dve.wait_ge(mod_ok, 1)
            dve.wait_ge(const_in, 4 * 16)
            dve.wait_ge(x_in, 16)
            norm_d(na, 0)
            norm_rstd(na, 0, 6)
            norm_rest(0)
            split(0)

            def tail(t, m):
                nc.vector.reciprocal(ch(wc_t, m), ch(wc_t, m)).then_inc(a.rcp_ok, 1)
                dve.wait_ge(a.rcp_ok, NC * t + m + 1)
                dve.sem_inc(settled)
                nc.vector.tensor_tensor(ch(kv_t, m), ch(kv_t, m), ch(wc_t, m), ALU.mult).then_inc(a.y_ok, 1)

            def tile_a(t, first=False, last=False):
                u = t + 1
                if not last:
                    norm_d(na, u)
                if not first:
                    dve.wait_ge(a.den_ok, t)
                    dve.sem_inc(settled)
                    tail(t - 1, 0)
                dve.wait_ge(a.seed_k, t + 1)
                dve.sem_inc(settled)
                newton(rs_qk, nt_qk, b_qk, RMS_EPS, a.newton, 6 * t, a.rk_ok)
                if not first:
                    tail(t - 1, 1)
                if not last:
                    norm_rstd(na, u, 6)
                if not first:
                    tail(t - 1, 2)
                dve.wait_ge(a.seed_q, t + 1)
                dve.sem_inc(settled)
                newton(rs_qk, nt_qk, b_qk, RMS_EPS, a.newton, 6 * t + 3, a.rq_ok)
                if not first:
                    tail(t - 1, 3)
                dve.wait_ge(a.w_ok, t + 1)
                dve.sem_inc(settled)
                dve.wait_ge(a.qsum, t + 1)
                dve.sem_inc(settled)
                for m in range(NC):
                    dve.wait_ge(a.mm, NQKV * t + 2 * NC + m + 1)
                    dve.sem_inc(settled)
                    nc.vector.tensor_tensor(ch(wv_t, m), ch(k_t, m), bank[(2 * NC + m) % 6][:, :],
                                            ALU.mult).then_inc(a.wv_ok, 1)
                if first:
                    dve.wait_ge(carry_ok, 2)
                else:
                    dve.wait_ge(y_st, 16 * t)
                    dve.sem_inc(settled)
                    dve.wait_ge(a.carry, 2 * t)
                    dve.sem_inc(settled)
                for m in range(NC):
                    dve.wait_ge(a.wv_ok, NC * t + m + 1)
                    dve.sem_inc(settled)
                    nc.vector.tensor_tensor_scan(ch(kv_t, m), ch(wv_t, m), ch(wv_t, m), carry_kv[:, m:m + 1],
                                                 ALU.add, ALU.bypass).then_inc(a.scan_ok, 1)
                    nc.vector.tensor_tensor_scan(ch(wc_t, m), ch(k_t, m), ch(k_t, m), carry_w[:, m:m + 1],
                                                 ALU.add, ALU.bypass).then_inc(a.scan_ok, 1)
                dve.wait_ge(a.scan_ok, 2 * NC * (t + 1))
                dve.sem_inc(settled)
                keep = mod_t[:, t, 6 * NC:6 * NC + 1]
                nc.vector.tensor_scalar(carry_kv[:, :], rows(kv_t)[:, :, TT - 1], keep, None,
                                        ALU.mult).then_inc(a.carry, 1)
                nc.vector.tensor_scalar(carry_w[:, :], rows(wc_t)[:, :, TT - 1], keep, None,
                                        ALU.mult).then_inc(a.carry, 1)
                dve.wait_ge(a.carry, 2 * t + 2)
                dve.sem_inc(settled)
                nc.vector.tensor_scalar(wc_t[:, :], wc_t[:, :], 1e-06, None, ALU.add).then_inc(a.denp, 1)
                dve.wait_ge(a.e_ok, t + 1)
                dve.sem_inc(settled)
                dve.wait_ge(a.denp, t + 1)
                dve.sem_inc(settled)
                nc.vector.scalar_tensor_tensor(out=wc_t[:, :], in0=q_t[:, :], scalar=1.0, in1=wc_t[:, :],
                                               op0=ALU.add, op1=ALU.mult).then_inc(a.den_ok, 1)
                if not last:
                    norm_rest(u)
                    split(NC * u)
                else:
                    split(NC * NT)

            tile_a(0, first=True)
            with dve.Fori(1, LAST) as t:
                tile_a(t)
            tile_a(LAST, last=True)
            dve.wait_ge(a.den_ok, NT)
            for m in range(NC):
                tail(LAST, m)
            dve.wait_ge(y_st, 16 * NT)
            nc.vector.memset(gates_tok[:, :, :], 0.0).then_inc(ones_ok, 1)
            dve.wait_ge(ones_ok, 2)
            nc.vector.memset(gates_tok[:, :, 2 * E:NG], 1.0).then_inc(ones_ok, 1)

            GCH = 12

            def gating(u):
                n = [GCH * u]

                def then(ins):
                    n[0] = n[0] + 1
                    ins.then_inc(nd.gate_chain, 1)
                    dve.wait_ge(nd.gate_chain, n[0])
                    dve.sem_inc(settled)

                def first_max(onehot, src, top):
                    then(nc.vector.reduce_max(top[:, :], src[:, :, :], axis=AX_X))
                    then(nc.vector.tensor_tensor(eq[:, :, :], src[:, :, :], wide(top), ALU.is_equal))
                    then(nc.vector.tensor_tensor(eq[:, :, :], eq[:, :, :], ranks, ALU.mult))
                    then(nc.vector.reduce_max(fst[:, :], eq[:, :, :], axis=AX_X))
                    then(nc.vector.tensor_tensor(onehot[:, :, :], eq[:, :, :], wide(fst), ALU.is_equal))

                dve.wait_ge(nd.logit_mm, u + 1)
                dve.sem_inc(settled)
                then(nc.vector.tensor_copy(lg[:, :, :], b_x[:, 0:NSUB * E].rearrange("p (s e) -> p s e", s=NSUB)))
                first_max(top1, lg, m1)
                then(nc.vector.scalar_tensor_tensor(out=lg2[:, :, :], in0=top1[:, :, :], scalar=-3.0e38,
                                                    in1=lg[:, :, :], op0=ALU.mult, op1=ALU.add))
                first_max(top2, lg2, m2)
                nc.vector.tensor_tensor(m2[:, :], m2[:, :], m1[:, :], ALU.subtract).then_inc(nd.top_ok, 1)

            def gates(u):
                k = [0]

                def then(ins):
                    k[0] += 1
                    ins.then_inc(gate_fin, 1)
                    dve.wait_ge(gate_fin, 7 * u + k[0])
                    dve.sem_inc(settled)

                dve.wait_ge(nd.e_ok, u + 1)
                dve.sem_inc(settled)
                then(nc.vector.tensor_scalar(g1[:, :], g2[:, :], 1.0, None, ALU.add))
                then(nc.vector.reciprocal(g1[:, :], g1[:, :]))
                then(nc.vector.tensor_tensor(g2[:, :], g2[:, :], g1[:, :], ALU.mult))
                then(nc.vector.tensor_tensor(top1[:, :, :], top1[:, :, :], wide(g1), ALU.mult))
                then(nc.vector.tensor_tensor(top2[:, :, :], top2[:, :, :], wide(g2), ALU.mult))
                then(nc.vector.tensor_tensor(top1[:, :, :], top1[:, :, :], top2[:, :, :], ALU.add))
                then(nc.vector.tensor_copy(gates_tok[:, :, 0:E].bitcast(F32R), top1[:, :, :]))
                nc.vector.tensor_tensor(gates_tok[:, :, E:2 * E], top1[:, :, :], gates_tok[:, :, 0:E],
                                        ALU.subtract).then_inc(nd.gt_ok, 1)

            def wide(t):
                return t[:, :].rearrange("p (s o) -> p s o", o=1).broadcast_to([P, NSUB, E])

            ranks = rank_t[:, :].rearrange("p (o e) -> p o e", o=1).broadcast_to([P, NSUB, E])

            def hooks(h, s, u):
                if s == h["mean"]:
                    norm_d(nd, u)
                if s == h["var"]:
                    norm_rstd(nd, u, 3)
                if s == h["logit"]:
                    gating(u)
                if s == h["e"]:
                    gates(u)

            def block_(p, t, s):
                f, nb = ffn[p], NB[p]
                routed = s < N_ROUTED[p]
                if UPS[p] == 2:
                    dve.wait_ge(f.up, 2 * (nb * t + s) + 2)
                    dve.sem_inc(settled)
                dve.wait_ge(f.act_ok, nb * t + s + 1)
                dve.sem_inc(settled)
                if UPS[p] == 2:
                    other = bank[4 + (2 * s + 1) % 3][:, :]
                elif routed:
                    per_tile = N_ROUTED[p] // 2 + (1 if p == "e" else 0)
                    dve.wait_ge(f.gb, per_tile * t + s // 2 + 1 + (1 if p == "e" and s >= 4 else 0))
                    dve.sem_inc(settled)
                    other = bank[6][:, :]
                if UPS[p] == 2 or routed:
                    nc.vector.tensor_tensor(s_t[:, s % 2, :], act_t[:, s % 2, :], other, ALU.mult).then_inc(f.s_ok, 1)
                else:
                    nc.vector.tensor_copy(s_t[:, s % 2, :], act_t[:, s % 2, :]).then_inc(f.s_ok, 1)
                dve.wait_ge(f.sh_ok, nb * t + s + 1)
                dve.sem_inc(settled)
                nc.vector.tensor_tensor(s_lo[:, s % 3, :], s_t[:, s % 2, :], s_hi[:, s % 3, :].bitcast(F32),
                                        ALU.subtract).then_inc(f.sl_ok, 1)

            def tile(p, t, last=False):
                f, nb = ffn[p], NB[p]
                for s in range(nb):
                    block_(p, t, s)
                    if p == "d" and not last:
                        hooks(HOOKS_D, s, t + 1)
                    if p == "c" and last:
                        hooks(HOOKS_C, s, 0)
                if not (last and p == "e"):
                    q, u = (NEXT[p], 0) if last else (p, t + 1)
                    split(NC * (NT * PASS[q] + u))
                dve.wait_ge(f.dn, nb * (t + 1))
                dve.sem_inc(settled)
                dve.wait_ge(r_in, 16 * (NT * PASS[p] + t + 1))
                dve.sem_inc(settled)
                for m in range(NC):
                    nc.vector.scalar_tensor_tensor(out=ch(r_t, m), in0=bank[m][:, :], scalar=vec(t, GAIN[p], m),
                                                   in1=ch(r_t, m), op0=ALU.mult, op1=ALU.add).then_inc(f.ev_ok, 1)

            for p in "bcde":
                with dve.Fori(0, LAST) as t:
                    tile(p, t)
                tile(p, LAST, last=True)


def kernel(**inputs):
    import concourse.bacc as bacc
    import numpy as np
    from concourse.bass_utils import run_bass_kernel_spmd

    x = np.ascontiguousarray(inputs["L0_attn_x"])
    B, S, D = x.shape
    nc_, nt = D // P, B * S // TT
    E, _, H = inputs["L0_ffn_w1"].shape

    def blocks(w, rows_, cols):
        return np.asarray(w).reshape(rows_ // P, P, cols // P, P).transpose(2, 0, 1, 3)

    w_qkv = blocks(np.asarray(inputs["L0_attn_w_qkv"]).T, D, 3 * D)
    w_qkv = np.concatenate([w_qkv[nc_:2 * nc_], w_qkv[0:nc_], w_qkv[2 * nc_:]])
    w_qkv = w_qkv.reshape(nc_, 3 * nc_, P, P).transpose(0, 2, 1, 3).reshape(nc_, P, 3 * nc_ * P)
    swi = np.asarray(inputs["L0_attn_w_swiglu"])
    F = swi.shape[0] // 2
    up = blocks(swi.T, D, 2 * F)
    down = np.asarray(inputs["L0_attn_w_out"]).T.reshape(F // P, P, nc_, P).transpose(0, 2, 1, 3)
    w_swi = np.concatenate([up[F // P:], up[:F // P], down], axis=1)
    w_swi = w_swi.transpose(0, 2, 1, 3).reshape(F // P, P, 3 * nc_ * P)
    w1 = np.concatenate([blocks(w, D, H) for w in np.asarray(inputs["L0_ffn_w1"])]
                        + [blocks(inputs["L0_ffn_shared_w1"], D, D)])
    w2 = np.concatenate([np.asarray(inputs["L0_ffn_w2"]).reshape(E * H, D), np.asarray(inputs["L0_ffn_shared_w2"])])
    w2 = w2.reshape(-1, P, nc_, P).transpose(0, 2, 1, 3)
    w_moe = np.concatenate([w1, w2], axis=1).transpose(0, 2, 1, 3).reshape(-1, P, 2 * nc_ * P)
    b1 = np.concatenate([np.asarray(inputs["L0_ffn_b1"]).reshape(-1), np.asarray(inputs["L0_ffn_shared_b1"])])
    b2 = np.asarray(inputs["L0_ffn_b2"])
    b2 = np.concatenate([b2, b2, np.asarray(inputs["L0_ffn_shared_b2"])[None]])
    c = np.asarray(inputs["L0_c"]).reshape(B, nc_, P).transpose(2, 1, 0).reshape(P, nc_ * B)
    wmod = np.asarray(inputs["L0_wmod"]).reshape(nc_, P, 6, D).transpose(2, 1, 0, 3).reshape(6, P, nc_ * D)
    gate_w = np.asarray(inputs["L0_ffn_gate_w"]).reshape(nc_, P, E).transpose(1, 0, 2).reshape(P, nc_ * E)
    arrays = {
        "x": x.reshape(nt, TT, nc_, P).transpose(0, 3, 2, 1).reshape(nt, P, nc_ * TT),
        "c": c, "wmod": wmod, "w_qkv": w_qkv, "w_swi": w_swi, "w_moe": w_moe,
        "b1": b1.reshape(-1, P).T, "b2": b2, "gate_w": gate_w,
        "select": np.repeat(np.concatenate([np.eye(E), np.eye(E)]), P, axis=1).astype(np.float32),
        "ident": np.eye(P, dtype=np.float32),
        "rank": np.tile(np.arange(E, 0, -1, dtype=np.float32), (P, 1)),
    }
    arrays = {k: np.ascontiguousarray(v) for k, v in arrays.items()}
    nc = bacc.Bacc("TRN2", target_bir_lowering=False, num_devices=1)
    args = [nc.dram_tensor(k, v.shape, mybir.dt.from_np(v.dtype), kind="ExternalInput").ap()
            for k, v in arrays.items()]
    out = nc.dram_tensor("out", (nt, P, nc_ * TT), F32, kind="ExternalOutput").ap()
    build(nc, *args, out)
    r = run_bass_kernel_spmd(nc, [arrays], core_ids=[0])
    got = np.asarray(r.results[0]["out"]).reshape(nt, P, nc_, TT).transpose(0, 3, 2, 1)
    return np.ascontiguousarray(got).reshape(B, S, D)
```

```python
from collections import namedtuple
from contextlib import ExitStack
import math


import concourse.bass as bass
from concourse import mybir

F32 = mybir.dt.float32
F32R = mybir.dt.float32r
ALU = mybir.AluOpType
ACT = mybir.ActivationFunctionType
AX_X = mybir.AxisListType.X

P = 128
TT = 512
LN_EPS = 1e-05
W_EPS = 1e-06
RMS_EPS = 1.1920929e-07
SEED_SCALE = 2.0 ** -16
EXP_LN_SET = "natural_log_exp_and_others"
SILU_SET = "silu_and_others"
GELU_SET = "gelu_and_others"
SA, CA, GA, SB, CB, GB = range(6)


def build(nc, x, c, wmod, w_qkv, w_swi, w_moe, b1, b2, gate_w, select, ident, rank, out):
    NT = x.shape[0]
    D = x.shape[2] // TT * P
    NC = D // P
    NB_SEQ = c.shape[1] // NC
    T_SEQ = NT // NB_SEQ
    E = gate_w.shape[1] // NC
    NG = 2 * E + 1
    NQKV = 3 * NC
    ROUTED = w_moe.shape[0] - NC
    SWI_W = w_swi.shape[2]
    MOE_W = w_moe.shape[2]
    QKV_W = NC * P
    CHW = NC * TT
    W_COLS = 8 * SWI_W
    NSUB = TT // P
    LAST = NT - 1
    NB_SWI = w_swi.shape[0] // 2
    NB_MOE = w_moe.shape[0] // 2
    assert NC == 4 and NB_SEQ == 2 and NB_SWI * SWI_W == W_COLS and NB_MOE * MOE_W <= W_COLS

    QKV_PIECES = w_qkv.shape[0]
    swi_col = [(j + NB_SWI // 2) % NB_SWI * SWI_W for j in range(NB_SWI)]
    moe_col = [(swi_col[0] + j * MOE_W) % W_COLS for j in range(NB_MOE)]
    pieces = [(w_qkv[i], i * SWI_W, SWI_W) for i in range(QKV_PIECES)]
    B0 = len(pieces)
    pieces += [(w_swi[j], swi_col[j], SWI_W) for j in range(NB_SWI)]
    C0 = len(pieces)
    pieces += [(w_swi[NB_SWI + j], swi_col[j], SWI_W) for j in range(NB_SWI)]
    D0 = len(pieces)
    pieces += [(w_moe[j], moe_col[j], MOE_W) for j in range(NB_MOE)]
    E0 = len(pieces)
    pieces += [(w_moe[NB_MOE + j], moe_col[j], MOE_W) for j in range(NB_MOE)]

    y_dram = nc.dram_tensor("y_scratch", (NT, P, CHW), F32, kind="Internal").ap()
    ra_dram = nc.dram_tensor("residual_a", (NT, P, CHW), F32, kind="Internal").ap()
    rb_dram = nc.dram_tensor("residual_b", (NT, P, CHW), F32, kind="Internal").ap()
    g_dram = nc.dram_tensor("gate_scratch", (NT, NG, TT), F32, kind="Internal").ap()

    ctx = ExitStack()
    with ctx:
        def sb(name, shape, dt=F32):
            return ctx.enter_context(nc.sbuf_tensor(name, shape, dt))

        def sem(name):
            return ctx.enter_context(nc.semaphore(name))

        def sems(suffix, names):
            return namedtuple("Sems", names)(*[sem(f"{n}_{suffix}") for n in names.split()])

        w_hi = sb("w_hi", [P, W_COLS], F32R)
        w_lo = sb("w_lo", [P, W_COLS], F32R)
        raw = [sb(f"raw{i}", [P, SWI_W]) for i in range(2)]
        x_t = sb("x_t", [P, CHW])
        r_t = sb("r_t", [P, CHW])
        sq_t = sb("sq_t", [P, CHW])
        sum_x = sb("sum_x", [P, TT])
        sum_qk = sb("sum_qk", [P, TT])
        rs_x = sb("rs_x", [P, TT])
        nt_x = sb("nt_x", [P, TT])
        rs_qk = sb("rs_qk", [P, TT])
        nt_qk = sum_qk
        x_hi = sb("x_hi", [P, CHW], F32R)
        x_lo = sb("x_lo", [P, CHW], F32R)
        mod_t = sb("mod_t", [P, NT, 6 * NC + 2])
        mod_raw = sb("mod_raw", [P, 6 * NC * NB_SEQ])
        mod_tmp = sb("mod_tmp", [P, 2 * NC * NB_SEQ])
        c_t = sb("c_t", [P, NC * NB_SEQ])
        c_e = sb("c_e", [P, NC * NB_SEQ])
        id2 = sb("id2", [NB_SEQ, NB_SEQ])
        mean_w = sb("mean_w", [P, P])
        carry_kv = sb("carry_kv", [P, NC])
        carry_w = sb("carry_w", [P, NC])
        eps_t = sb("eps_t", [P, 3])
        eps_ln, eps_rms, seed_shift = eps_t[:, 0:1], eps_t[:, 1:2], eps_t[:, 2:3]

        with ExitStack() as only_a:
            def sa_(name):
                return only_a.enter_context(nc.sbuf_tensor(name, [P, CHW], F32))
            x_a = sa_("x_a")
            k_t, wv_t, q_t, kv_t, wc_t = [sa_(n) for n in ("k_t", "wv_t", "q_t", "kv_t", "wc_t")]
        act_t = sb("act_t", [P, 2, TT])
        s_t = sb("s_t", [P, 2, TT])
        s_hi = sb("s_hi", [P, 3, TT], F32R)
        s_lo = sb("s_lo", [P, 3, TT], F32R)
        ident_t = sb("ident_t", [P, P])
        b1_t = sb("b1_t", [P, w_moe.shape[0]])
        gw_t = sb("gw_t", [P, NC * E])
        rank_t = sb("rank_t", [P, E])
        g_next = sb("g_next", [NG, TT])
        g_rows = sb("g_rows", [NG, TT], F32R)
        sel_raw = sb("sel_raw", [2 * E, E * P])
        sel_t = sb("sel_t", [2 * E, E * P], F32R)
        b2_raw = sb("b2_raw", [NG, D])
        b2_hi = sb("b2_hi", [NG, D], F32R)
        b2_lo = sb("b2_lo", [NG, D], F32R)
        gates_tok = sb("gates_tok", [P, NSUB, P])
        lg = sb("lg", [P, NSUB, E])
        eq = sb("eq", [P, NSUB, E])
        top1 = sb("top1", [P, NSUB, E])
        lg2 = sb("lg2", [P, NSUB, E])
        top2 = sb("top2", [P, NSUB, E])
        m1 = sb("m1", [P, NSUB])
        m2 = sb("m2", [P, NSUB])
        fst = sb("fst", [P, NSUB])
        g1 = sb("g1", [P, NSUB])
        g2 = sb("g2", [P, NSUB])
        bank = [ctx.enter_context(nc.psum_tensor(f"bank{i}", [P, TT], F32)) for i in range(8)]
        b_qk, b_x = bank[6], bank[7]

        const_in, c_in, sel_in = sem("const_in"), sem("c_in"), sem("sel_in")
        wmod_in = [sem(f"wmod_in{v}") for v in range(6)]
        raw_in = [sem("raw_in0"), sem("raw_in1")]
        w_hi_ok, w_ok = sem("w_hi_ok"), sem("w_ok")
        ones_ok, carry_ok, keep_ok = sem("ones_ok"), sem("carry_ok"), sem("keep_ok")
        c_exp, c_silu, id2_in = sem("c_exp"), sem("c_silu"), sem("id2_in")
        mod_mm, mod_row, mod_tr, mod_cp, mod_ok = [sem(n) for n in ("mod_mm", "mod_row", "mod_tr", "mod_cp", "mod_ok")]
        xa_in, x_in, r_in, r_st = sem("xa_in"), sem("x_in"), sem("r_in"), sem("r_st")
        xh_ok, xl_ok = sem("xh_ok"), sem("xl_ok")
        y_st, h_st, g_st, out_st = sem("y_st"), sem("h_st"), sem("g_st"), sem("out_st")
        g_in = sem("g_in")
        sel_ok = sem("sel_ok")
        settled = sem("settled")
        setup_v = sem("setup_v")
        LN = "sum0 mean_mm d_ok dsq_ok sum1 var_mm ln_ok seed_ok newton rstd_ok dr_ok h_ok half"
        na = sems("norm_a", LN + " hsq_ok sum2 rms_mm rrms_ok n_ok r_ok halfr lnr_ok seedr_ok newtonr")
        nd = sems("norm_d", LN + " logit_mm top_ok e_ok gate_chain gt_ok tr_mm gp_ok")
        a = sems("qkv", "mm x_used kq_ev ksum k_mm ln_k seed_k newton rk_ok kn_ok w_ok qsum q_mm ln_q seed_q rq_ok qn_ok "
                      "e_ok wv_ok scan_ok carry den_ok ln_y seed_y dr_y y0_ok y_ok halfqk")
        ffn = {p: sems(p, "up act_ok s_ok sh_ok sl_ok dn ev_ok gb") for p in "bcde"}
        g_cp, gate_fin = sem("g_cp"), sem("gate_fin")

        PASS = {"a": 0, "b": 1, "c": 2, "d": 3, "e": 4}
        NB = {"b": NB_SWI, "c": NB_SWI, "d": NB_MOE, "e": NB_MOE}
        W0 = {"b": B0, "c": C0, "d": D0, "e": E0}
        UPS = {"b": 2, "c": 2, "d": 1, "e": 1}
        GAIN = {"b": GA, "c": GA, "d": GB, "e": GB}
        NEXT = {"a": "b", "b": "c", "c": "d", "d": "e"}
        N_ROUTED = {"b": 0, "c": 0, "d": NB_MOE, "e": ROUTED - NB_MOE}
        HOOKS_C = dict(mean=2, sq=2, var=4, h=5, logit=6, e=7, tr=9)
        HOOKS_D = dict(mean=4, sq=4, var=6, h=7, logit=8, e=9, tr=11)

        def ch(t, m):
            return t[:, m * TT:(m + 1) * TT]

        def rows(t):
            return t[:, :].rearrange("p (c n) -> p c n", c=NC)

        def over_chunks(t):
            return t[:, :].rearrange("p (o n) -> p o n", o=1).broadcast_to([P, NC, TT])

        def vec(t, v, m):
            return mod_t[:, t, v * NC + m:v * NC + m + 1]

        wmod_bufs = [k_t, q_t, wv_t, kv_t, wc_t, k_t]

        block = ctx.enter_context(nc.Block())

        @block.sync
        def _(sp):
            def piece(i):
                if i >= 2:
                    sp.wait_ge(w_ok, i - 1)
                src, _, n = pieces[i]
                sp.dma_start(raw[i % 2][:, 0:n], src).then_inc(raw_in[i % 2], 16)

            def load_x(src, t):
                sp.dma_start(x_t[:, :], src[t]).then_inc(x_in, 16)

            def load_r(src, t):
                sp.dma_start(r_t[:, :], src[t]).then_inc(r_in, 16)

            def load_xa(t):
                sp.dma_start(x_a[:, :], x[t]).then_inc(xa_in, 16)

            sp.dma_start(c_t[:, :], c).then_inc(c_in, 16)
            load_xa(0)
            sp.dma_start(id2[:, :], ident[0:NB_SEQ, 0:NB_SEQ]).then_inc(id2_in, 16)
            for v in range(3):
                sp.dma_start(wmod_bufs[v][:, :], wmod[v]).then_inc(wmod_in[v], 16)
            piece(0)
            piece(1)
            for v in (3, 4):
                sp.dma_start(wmod_bufs[v][:, :], wmod[v]).then_inc(wmod_in[v], 16)
            load_r(x, 0)
            sp.wait_ge(mod_tr, 1)
            sp.dma_start(wmod_bufs[5][:, :], wmod[5]).then_inc(wmod_in[5], 16)
            piece(2)
            sp.wait_ge(na.dr_ok, 1)
            load_xa(1)
            piece(3)
            sp.wait_ge(na.r_ok, NC)
            sp.dma_start(ra_dram[0], r_t[:, :]).then_inc(r_st, 16)
            sp.wait_ge(r_st, 16)
            load_r(x, 1)
            piece(4)
            piece(5)

            def tile_a(t, stage1=True, stage2=True, tail=True):
                u = t + 1
                if stage1:
                    sp.wait_ge(na.dr_ok, u + 1)
                    sp.sem_inc(settled)
                    load_xa(u + 1)
                if stage2:
                    sp.wait_ge(na.r_ok, NC * (u + 1))
                    sp.sem_inc(settled)
                    sp.dma_start(ra_dram[u], r_t[:, :]).then_inc(r_st, 16)
                    sp.wait_ge(r_st, 16 * (u + 1))
                    sp.sem_inc(settled)
                    if stage1:
                        load_r(x, u + 1)
                    else:
                        load_r(ra_dram, 0)
                if tail:
                    sp.wait_ge(a.y_ok, t)
                    sp.sem_inc(settled)
                    sp.dma_start(y_dram[t - 1], kv_t[:, :]).then_inc(y_st, 16)

            tile_a(0, tail=False)
            with sp.Fori(1, LAST - 1) as t:
                tile_a(t)
            piece(6)
            tile_a(LAST - 1, stage1=False)
            piece(7)
            sp.wait_ge(xl_ok, NC * NT)
            sp.wait_ge(y_st, 16)
            load_x(y_dram, 0)
            tile_a(LAST, stage1=False, stage2=False)
            for i in range(8, C0):
                piece(i)
            sp.wait_ge(a.y_ok, NT)
            sp.dma_start(y_dram[LAST], kv_t[:, :]).then_inc(y_st, 16)
            sp.wait_ge(y_st, 16 * NT)
            sp.dma_start(sel_raw[:, :], select).then_inc(sel_in, 16)
            sp.dma_start(b2_raw[:, :], b2).then_inc(sel_in, 16)
            for dst, src in ((ident_t, ident), (b1_t, b1), (gw_t, gate_w), (rank_t, rank)):
                sp.dma_start(dst[:, :], src).then_inc(const_in, 16)

            X_SRC = {"b": y_dram, "c": y_dram, "d": ra_dram, "e": y_dram}
            R_SRC = {"b": ra_dram, "c": rb_dram, "d": ra_dram, "e": rb_dram}
            R_DST = {"b": rb_dram, "c": ra_dram, "d": rb_dram, "e": out}

            def next_x(p, t):
                sp.wait_ge(xl_ok, NC * (NT * PASS[p] + t))
                if p == "b":
                    sp.sem_inc(settled)
                    sp.wait_ge(y_st, 16 * (t + 1))
                if p == "d":
                    sp.sem_inc(settled)
                    sp.wait_ge(r_st, 16 * (2 * NT + t + 1))
                    sp.sem_inc(settled)
                    sp.wait_ge(h_st, 16 * t)
                if p == "e":
                    sp.sem_inc(settled)
                    sp.wait_ge(h_st, 16 * NT)
                    sp.wait_ge(g_cp, NT + t)
                    sp.sem_inc(settled)
                    sp.wait_ge(g_st, 16 * NT)
                sp.sem_inc(settled)
                load_x(X_SRC[p], t)
                if p == "e":
                    sp.dma_start(g_next[:, :], g_dram[t]).then_inc(g_in, 16)

            def store_h(t):
                sp.wait_ge(nd.h_ok, NC * (t + 1))
                sp.sem_inc(settled)
                sp.dma_start(y_dram[t], x_t[:, :]).then_inc(h_st, 16)
                sp.wait_ge(nd.gp_ok, t + 1)
                sp.sem_inc(settled)
                sp.dma_start(g_dram[t], g_next[:, :]).then_inc(g_st, 16)

            def tile(p, t, last=False):
                if not last:
                    next_x(p, t + 1)
                elif p != "e":
                    next_x(NEXT[p], 0)
                if last and p != "e":
                    n0 = W0[NEXT[p]]
                    for i in range(n0, n0 + NB[NEXT[p]]):
                        piece(i)
                if p == "d" and not last:
                    store_h(t + 1)
                if p == "c" and last:
                    store_h(0)
                sp.wait_ge(ffn[p].ev_ok, NC * (t + 1))
                sp.sem_inc(settled)
                if p == "e":
                    sp.dma_start(R_DST[p][t], r_t[:, :]).then_inc(out_st, 16)
                    sp.wait_ge(out_st, 16 * (t + 1))
                else:
                    sp.dma_start(R_DST[p][t], r_t[:, :]).then_inc(r_st, 16)
                    sp.wait_ge(r_st, 16 * (NT * PASS[p] + t + 1))
                sp.sem_inc(settled)
                if not last:
                    load_r(R_SRC[p], t + 1)
                elif p != "e":
                    load_r(R_SRC[NEXT[p]], 0)

            for p in "bcde":
                with sp.Fori(0, LAST) as t:
                    tile(p, t)
                tile(p, LAST, last=True)
            for s, n in ((y_st, 16 * NT), (h_st, 16 * NT), (g_st, 16 * NT), (r_st, 4 * 16 * NT), (out_st, 16 * NT)):
                sp.wait_ge(s, n)

        @block.gpsimd
        def _(pool):
            def piece(i):
                _, col, n = pieces[i]
                pool.wait_ge(raw_in[i % 2], 16 * (i // 2 + 1))
                src = raw[i % 2][:, 0:n]
                nc.gpsimd.tensor_scalar(w_hi[:, col:col + n], src, 1.0, 1.0, ALU.mult, ALU.mult).then_inc(w_hi_ok, 1)
                pool.wait_ge(w_hi_ok, i + 1)
                nc.gpsimd.tensor_tensor(w_lo[:, col:col + n], src, w_hi[:, col:col + n].bitcast(F32),
                                        ALU.subtract).then_inc(w_ok, 1)

            def chunk_sum(dst, src, pair, half_done, n, done):
                nc.gpsimd.tensor_tensor(pair[:, 0:2 * TT], src[:, 0:CHW // 2], src[:, CHW // 2:CHW],
                                        ALU.add).then_inc(half_done, 1)
                pool.wait_ge(half_done, n + 1)
                nc.gpsimd.tensor_tensor(dst[:, :], pair[:, 0:TT], pair[:, TT:2 * TT],
                                        ALU.add).then_inc(done, 1)

            def sum_x0(n, src, arrived, count, u):
                pool.wait_ge(arrived, count)
                chunk_sum(sum_x, src, sq_t, n.half, 2 * u, n.sum0)

            def sum_d(n, u):
                pool.wait_ge(n.dsq_ok, u + 1)
                chunk_sum(sum_x, sq_t, sq_t, n.half, 2 * u + 1, n.sum1)

            def sum_h(u):
                pool.wait_ge(na.hsq_ok, u + 1)
                chunk_sum(sum_x, sq_t, sq_t, na.halfr, u, na.sum2)

            sum_x0(na, x_a, xa_in, 16, 0)
            sum_d(na, 0)
            piece(0)
            piece(1)
            sum_h(0)
            piece(2)
            pool.wait_ge(na.rms_mm, 1)
            sum_x0(na, x_a, xa_in, 32, 1)
            piece(3)
            sum_d(na, 1)

            def tile_a(t, stage1=True, stage2=True):
                u = t + 1
                pool.wait_ge(a.kq_ev, 2 * NC * t + NC)
                chunk_sum(sum_qk, wv_t, wv_t, a.halfqk, 2 * t, a.ksum)
                if stage2:
                    sum_h(u)
                if stage1:
                    pool.wait_ge(na.rms_mm, u + 1)
                    sum_x0(na, x_a, xa_in, 16 * (u + 2), u + 1)
                pool.wait_ge(a.rk_ok, t + 1)
                nc.gpsimd.tensor_tensor(rows(k_t), rows(k_t), over_chunks(rs_qk), ALU.mult).then_inc(a.kn_ok, 1)
                pool.wait_ge(a.kq_ev, 2 * NC * (t + 1))
                sq = wv_t if stage2 else sq_t
                chunk_sum(sum_qk, sq, sq, a.halfqk, 2 * t + 1, a.qsum)
                if stage1:
                    sum_d(na, u + 1)
                pool.wait_ge(a.rq_ok, t + 1)
                nc.gpsimd.tensor_tensor(rows(q_t), rows(q_t), over_chunks(rs_qk), ALU.mult).then_inc(a.qn_ok, 1)

            tile_a(0)
            piece(4)
            with pool.Fori(1, LAST - 1) as t:
                tile_a(t)
            tile_a(LAST - 1, stage1=False)
            piece(5)
            tile_a(LAST, stage1=False, stage2=False)
            piece(6)
            piece(7)
            pool.wait_ge(a.x_used, NC * NT)
            for i in range(B0 + NB_SWI // 2, C0):
                piece(i)
            pool.wait_ge(sel_in, 32)
            nc.gpsimd.tensor_scalar(sel_t[:, :], sel_raw[:, :], 1.0, None, ALU.mult).then_inc(sel_ok, 1)
            nc.gpsimd.tensor_scalar(b2_hi[:, :], b2_raw[:, :], 1.0, None, ALU.mult).then_inc(sel_ok, 1)
            pool.wait_ge(sel_ok, 2)
            nc.gpsimd.tensor_tensor(b2_lo[:, :], b2_raw[:, :], b2_hi[:, :].bitcast(F32),
                                    ALU.subtract).then_inc(sel_ok, 1)

            def freed_by(col, n, cols, width):
                return max(j for j, k in enumerate(cols) if k < col + n and col < k + width)

            for j in range(NB_SWI):
                pool.wait_ge(ffn["b"].dn, NB_SWI * LAST + j + 1)
                piece(C0 + j)
            for j in range(NB_MOE):
                if j == 0:
                    sum_x0(nd, x_t, x_in, 16 * (2 * NT + 1), 0)
                if j == 1:
                    sum_d(nd, 0)
                pool.wait_ge(ffn["c"].dn, NB_SWI * LAST + freed_by(moe_col[j], MOE_W, swi_col, SWI_W) + 1)
                piece(D0 + j)
            with pool.Fori(0, LAST) as t:
                pool.wait_ge(nd.var_mm, t + 1)
                sum_x0(nd, x_t, x_in, 16 * (2 * NT + t + 2), t + 1)
                sum_d(nd, t + 1)
            for j in range(NB_MOE):
                pool.wait_ge(ffn["d"].dn, NB_MOE * LAST + j + 1)
                piece(E0 + j)

        @block.tensor
        def _(pe):
            def product(dst, rhs_hi, rhs_lo, col, start, stop):
                nc.tensor.matmul(dst, w_hi[:, col:col + P], rhs_hi, start=start, stop=False)
                nc.tensor.matmul(dst, w_hi[:, col:col + P], rhs_lo, start=False, stop=False)
                return nc.tensor.matmul(dst, w_lo[:, col:col + P], rhs_hi, start=False, stop=stop)

            def from_x(dst, col, first_of_tile=None):
                for m in range(NC):
                    if first_of_tile is not None:
                        pe.wait_ge(xl_ok, first_of_tile + m + 1)
                    ins = product(dst, ch(x_hi, m), ch(x_lo, m), col + m * P, m == 0, m == NC - 1)
                return ins

            def mean(dst, src):
                return nc.tensor.matmul(dst[:, :], mean_w[:, :], src[:, :], start=True, stop=True)

            def modulate(v):
                pe.wait_ge(wmod_in[v], 16)
                for k in range(NC):
                    ins = nc.tensor.matmul(bank[v % 6][0:NB_SEQ, :], c_t[:, k * NB_SEQ:(k + 1) * NB_SEQ],
                                           wmod_bufs[v][:, k * D:(k + 1) * D], start=(k == 0), stop=(k == NC - 1))
                ins.then_inc(mod_mm, 1)

            def rows_to_columns(v):
                pe.wait_ge(mod_row, v + 1)
                for m in range(NC):
                    at = (v * NC + m) * NB_SEQ
                    ins = nc.tensor.transpose(b_qk[:, at:at + NB_SEQ], wmod_bufs[v][0:NB_SEQ, m * P:(m + 1) * P],
                                              id2[:, :])
                ins.then_inc(mod_tr, 1)

            def norm_mean(n, u):
                pe.wait_ge(n.sum0, u + 1)
                mean(b_x, sum_x).then_inc(n.mean_mm, 1)

            def norm_var(n, u):
                pe.wait_ge(n.sum1, u + 1)
                mean(b_x, sum_x).then_inc(n.var_mm, 1)

            def norm_rms(u):
                pe.wait_ge(na.sum2, u + 1)
                mean(b_x, sum_x).then_inc(na.rms_mm, 1)

            pe.wait_ge(ones_ok, 1)
            norm_mean(na, 0)
            pe.wait_ge(c_silu, 1)
            modulate(0)
            modulate(1)
            pe.wait_ge(id2_in, 16)
            rows_to_columns(0)
            rows_to_columns(1)
            norm_var(na, 0)
            modulate(2)
            rows_to_columns(2)
            pe.wait_ge(mod_cp, 1)
            modulate(3)
            modulate(4)
            rows_to_columns(3)
            modulate(5)
            rows_to_columns(4)
            rows_to_columns(5)
            norm_rms(0)
            pe.wait_ge(na.rrms_ok, 1)
            norm_mean(na, 1)

            def tile_a(t, first=False, stage1=True, stage2=True):
                u = t + 1
                for o in range(NQKV - 3):
                    pe.wait_ge(w_ok, o // 3 + 1)
                    if o >= 6:
                        pe.wait_ge(a.kq_ev, 2 * NC * t + o - 5)
                    elif o >= 2 and not first:
                        pe.wait_ge(a.wv_ok, NC * (t - 1) + o - 1)
                    from_x(bank[o % 6][:, :], o * QKV_W, NC * t if o == 0 else None).then_inc(a.mm, 1)
                    if o == (3 if first else 0) and stage2:
                        norm_var(na, u)
                    if o == 5:
                        if first:
                            pe.wait_ge(mod_cp, 2)
                        pe.wait_ge(a.ksum, t + 1)
                        mean(b_qk, sum_qk).then_inc(a.k_mm, 1)
                    if o == 6 and stage2:
                        norm_rms(u)
                pe.wait_ge(w_ok, NC)
                pe.wait_ge(a.kq_ev, 2 * NC * t + NQKV - 6)
                for m in range(NC):
                    for o in range(NQKV - 3, NQKV):
                        ins = product(bank[o % 6][:, :], ch(x_hi, m), ch(x_lo, m), o * QKV_W + m * P,
                                      m == 0, m == NC - 1)
                        if m == NC - 1 and o < NQKV - 1:
                            ins.then_inc(a.mm, 1)
                    ins.then_inc(a.x_used, 1)
                    if m == 0 and stage1:
                        pe.wait_ge(na.rrms_ok, u + 1)
                        norm_mean(na, u + 1)
                    if m == (NC - 1 if stage2 else 1):
                        pe.wait_ge(a.qsum, t + 1)
                        pe.wait_ge(a.rk_ok, t + 1)
                        mean(b_qk, sum_qk).then_inc(a.q_mm, 1)

            tile_a(0, first=True)
            with pe.Fori(1, LAST - 1) as t:
                tile_a(t)
            tile_a(LAST - 1, stage1=False)
            tile_a(LAST, stage1=False, stage2=False)

            def logits(u):
                pe.wait_ge(nd.h_ok, NC * (u + 1))
                for s in range(NSUB):
                    for m in range(NC):
                        ins = nc.tensor.matmul(b_x[:, s * E:(s + 1) * E],
                                               x_t[:, m * TT + s * P:m * TT + (s + 1) * P],
                                               gw_t[:, m * E:(m + 1) * E], start=(m == 0), stop=(m == NC - 1))
                ins.then_inc(nd.logit_mm, 1)

            def gates_to_rows(u):
                pe.wait_ge(nd.gt_ok, u + 1)
                for s in range(NSUB):
                    ins = nc.tensor.transpose(b_x[:, s * P:(s + 1) * P], gates_tok[:, s, :], ident_t[:, :])
                ins.then_inc(nd.tr_mm, 1)

            def hooks(h, s, u):
                if s == h["mean"]:
                    norm_mean(nd, u)
                if s == h["var"]:
                    norm_var(nd, u)
                if s == h["logit"]:
                    logits(u)
                if s == h["tr"]:
                    gates_to_rows(u)

            def up(p, t, s):
                f, nb = ffn[p], NB[p]
                pe.wait_ge(w_ok, W0[p] + s + 1)
                first = NC * (NT * PASS[p] + t) if s == 0 else None
                if UPS[p] == 2:
                    for half in range(2):
                        o = 2 * s + half
                        if o >= 3:
                            read = f.s_ok if (o - 3) % 2 else f.act_ok
                            pe.wait_ge(read, nb * t + (o - 3) // 2 + 1)
                        from_x(bank[4 + o % 3][:, :], swi_col[s] + half * QKV_W,
                               first if half == 0 else None).then_inc(f.up, 1)
                    return
                if s >= 2:
                    pe.wait_ge(f.act_ok, nb * t + s - 1)
                from_x(bank[4 + s % 2][:, :], moe_col[s], first).then_inc(f.up, 1)
                if s % 2 == 0 and s < N_ROUTED[p]:
                    e = (0 if p == "d" else NB_MOE // 2) + s // 2
                    if s == 0:
                        pe.wait_ge(g_cp, (NT if p == "e" else 0) + t + 1)
                        pe.wait_ge(sel_ok, 3)
                    if s > 0:
                        pe.wait_ge(f.s_ok, nb * t + s)
                    nc.tensor.matmul(bank[6][:, :], sel_t[:, e * P:(e + 1) * P], g_rows[0:2 * E, :],
                                     start=True, stop=True).then_inc(f.gb, 1)

            def down(p, t, s):
                f, nb = ffn[p], NB[p]
                pe.wait_ge(f.sl_ok, nb * t + s + 1)
                if s == 0:
                    if p == "e":
                        for m in range(NC):
                            for part in (b2_hi, b2_lo):
                                ins = nc.tensor.matmul(bank[m][:, :], part[:, m * P:(m + 1) * P], g_rows[:, :],
                                                       start=part is b2_hi, stop=False)
                        ins.then_inc(f.gb, 1)
                col = swi_col[s] + 2 * QKV_W if UPS[p] == 2 else moe_col[s] + QKV_W
                for m in range(NC):
                    ins = product(bank[m][:, :], s_hi[:, s % 3, :], s_lo[:, s % 3, :], col + m * P,
                                  s == 0 and p != "e", s == nb - 1)
                ins.then_inc(f.dn, 1)

            def tile(p, t, last=False):
                for s in range(NB[p] + 2):
                    if s < NB[p]:
                        up(p, t, s)
                    if s >= 2:
                        down(p, t, s - 2)
                    if p == "d" and not last:
                        hooks(HOOKS_D, s, t + 1)
                    if p == "c" and last:
                        hooks(HOOKS_C, s, 0)

            for p in "bcde":
                if p == "c":
                    pe.wait_ge(const_in, 4 * 16)
                if p == "b":
                    pe.wait_ge(a.wv_ok, NC * NT)
                    pe.wait_ge(a.kq_ev, 2 * NC * NT)
                    pe.wait_ge(a.rq_ok, NT)
                else:
                    prev = ffn[{"c": "b", "d": "c", "e": "d"}[p]]
                    nbp = NB[{"c": "b", "d": "c", "e": "d"}[p]]
                    pe.wait_ge(prev.s_ok, nbp * NT)
                with pe.Fori(0, LAST) as t:
                    tile(p, t)
                tile(p, LAST, last=True)

        @block.scalar
        def _(act):
            act.wait_ge(c_in, 16)
            nc.scalar.preload_act_table_set(EXP_LN_SET)
            nc.scalar.activation(c_e[:, :], c_t[:, :], ACT.Exp, scale=-1.0).then_inc(c_exp, 1)

            def rsqrt_seed(dst, square, src, eps, chain, n, seed_done):
                nc.scalar.activation(dst[:, :], src[:, :], ACT.Ln, bias=eps).then_inc(chain, 1)
                act.wait_ge(chain, 2 * n + 1)
                nc.scalar.activation(dst[:, :], dst[:, :], ACT.Exp, scale=-0.5).then_inc(chain, 1)
                act.wait_ge(chain, 2 * n + 2)
                nc.scalar.activation(square[:, :], dst[:, :], ACT.Square).then_inc(seed_done, 1)

            def split(ready, count, scale=1.0, used=None):
                act.wait_ge(ready, count)
                for m in range(NC):
                    if used is not None:
                        act.wait_ge(a.x_used, used + m + 1)
                    nc.scalar.activation(ch(x_hi, m), ch(x_t, m), ACT.Copy, scale=scale).then_inc(xh_ok, 1)

            def norm_sq(n, src, u):
                act.wait_ge(n.d_ok, u + 1)
                nc.scalar.activation(sq_t[:, :], src[:, :], ACT.Square).then_inc(n.dsq_ok, 1)

            def norm_seed(n, u):
                act.wait_ge(n.var_mm, u + 1)
                rsqrt_seed(rs_x, nt_x, b_x, eps_ln, n.ln_ok, u, n.seed_ok)

            def norm_h(n, u, c_vec, s_vec):
                act.wait_ge(n.dr_ok, u + 1)
                for m in range(NC):
                    nc.scalar.activation(ch(x_t, m), ch(x_t, m), ACT.Identity, bias=vec(u, s_vec, m),
                                         scale=vec(u, c_vec, m)).then_inc(n.h_ok, 1)

            def norm_hsq(u):
                act.wait_ge(na.h_ok, NC * (u + 1))
                nc.scalar.activation(sq_t[:, :], x_t[:, :], ACT.Square).then_inc(na.hsq_ok, 1)

            def norm_rseed(u):
                act.wait_ge(na.rms_mm, u + 1)
                rsqrt_seed(rs_x, nt_x, b_x, eps_rms, na.lnr_ok, u, na.seedr_ok)

            def square_out(m, o, dst, sq, t):
                act.wait_ge(a.mm, (NQKV - 1) * t + o + 1)
                nc.scalar.activation(ch(dst, m), bank[o % 6][:, :], ACT.Copy)
                nc.scalar.activation(ch(sq, m), bank[o % 6][:, :], ACT.Square).then_inc(a.kq_ev, 1)

            def take_rows(v):
                act.wait_ge(mod_mm, v + 1)
                nc.scalar.activation(wmod_bufs[v][0:NB_SEQ, 0:D], bank[v % 6][0:NB_SEQ, :], ACT.Copy).then_inc(mod_row, 1)

            norm_sq(na, x_a, 0)
            take_rows(0)
            take_rows(1)
            norm_seed(na, 0)
            take_rows(2)
            act.wait_ge(mod_ok, 1)
            norm_h(na, 0, CA, SA)
            norm_hsq(0)
            for v in (3, 4, 5):
                take_rows(v)
            norm_rseed(0)
            split(na.n_ok, 1, -0.5)
            norm_sq(na, x_a, 1)

            def tile_a(t, stage1=True, stage2=True, tail=True):
                u = t + 1
                if tail:
                    exp_q(t - 1)
                if stage2:
                    norm_seed(na, u)
                for m in range(NC):
                    if tail:
                        act.wait_ge(a.scan_ok, 2 * (NC * (t - 1) + m + 1))
                    square_out(m, m, k_t, wv_t, t)
                if stage2:
                    norm_h(na, u, CA, SA)
                    norm_hsq(u)
                if tail:
                    seed_y(t - 1)
                act.wait_ge(a.k_mm, t + 1)
                rsqrt_seed(rs_qk, nt_qk, b_qk, eps_rms, a.ln_k, t, a.seed_k)
                if stage2:
                    norm_rseed(u)
                if tail:
                    act.wait_ge(a.y0_ok, t)
                for m in range(NC):
                    square_out(m, NC + m, q_t, wv_t if stage2 else sq_t, t)
                act.wait_ge(a.kn_ok, t + 1)
                nc.scalar.activation(k_t[:, :], k_t[:, :], ACT.Exp, scale=-0.5).then_inc(a.w_ok, 1)
                if stage1:
                    norm_sq(na, x_a, u + 1)
                if stage2:
                    split(na.n_ok, u + 1, -0.5, NC * t)
                act.wait_ge(a.q_mm, t + 1)
                rsqrt_seed(rs_qk, nt_qk, b_qk, eps_rms, a.ln_q, t, a.seed_q)
                if not stage2:
                    split(x_in, 16, 1.0, NC * t)

            def exp_q(t):
                act.wait_ge(a.qn_ok, t + 1)
                nc.scalar.activation(q_t[:, :], q_t[:, :], ACT.Exp, scale=0.5).then_inc(a.e_ok, 1)

            def seed_y(t):
                act.wait_ge(a.den_ok, t + 1)
                nc.scalar.activation(q_t[:, :], wc_t[:, :], ACT.Ln, scale=SEED_SCALE).then_inc(a.ln_y, 1)
                act.wait_ge(a.ln_y, t + 1)
                nc.scalar.activation(q_t[:, :], q_t[:, :], ACT.Exp, scale=-1.0, bias=seed_shift).then_inc(a.seed_y, 1)

            tile_a(0, tail=False)
            with act.Fori(1, LAST - 1) as t:
                tile_a(t)
            tile_a(LAST - 1, stage1=False)
            tile_a(LAST, stage1=False, stage2=False)
            exp_q(LAST)

            def hooks(h, s, u, back_to):
                if s == h["sq"]:
                    norm_sq(nd, x_t, u)
                if s == h["var"]:
                    nc.scalar.preload_act_table_set(EXP_LN_SET)
                    norm_seed(nd, u)
                if s == h["h"]:
                    norm_h(nd, u, CB, SB)
                if s == h["e"]:
                    nc.scalar.preload_act_table_set(EXP_LN_SET)
                    act.wait_ge(nd.top_ok, u + 1)
                    nc.scalar.activation(g2[:, :], m2[:, :], ACT.Exp).then_inc(nd.e_ok, 1)
                if s in (h["var"], h["e"]):
                    nc.scalar.preload_act_table_set(back_to)

            def take_gates(u, first):
                act.wait_ge(nd.tr_mm, u + 1)
                if not first:
                    act.wait_ge(g_st, 16 * u)
                nc.scalar.activation(g_next[:, :], b_x[0:NG, :], ACT.Copy).then_inc(nd.gp_ok, 1)

            def block_(p, t, s):
                f, nb = ffn[p], NB[p]
                act.wait_ge(f.up, UPS[p] * (nb * t + s) + 1)
                if UPS[p] == 2:
                    nc.scalar.activation(act_t[:, s % 2, :], bank[4 + 2 * s % 3][:, :], ACT.Silu).then_inc(f.act_ok, 1)
                else:
                    j = s + (NB_MOE if p == "e" else 0)
                    nc.scalar.activation(act_t[:, s % 2, :], bank[4 + s % 2][:, :], ACT.Gelu,
                                         bias=b1_t[:, j:j + 1]).then_inc(f.act_ok, 1)
                act.wait_ge(f.s_ok, nb * t + s + 1)
                nc.scalar.activation(s_hi[:, s % 3, :], s_t[:, s % 2, :], ACT.Copy).then_inc(f.sh_ok, 1)

            def rows_of_gates(p, t):
                if p == "d":
                    act.wait_ge(nd.gp_ok, t + 1)
                else:
                    act.wait_ge(g_in, 16 * (t + 1))
                nc.scalar.activation(g_rows[:, :], g_next[:, :], ACT.Copy).then_inc(g_cp, 1)

            def tile(p, t, last=False, tail=False):
                f = ffn[p]
                for s in range(NB[p]):
                    block_(p, t, s)
                    if tail and s == 1:
                        nc.scalar.preload_act_table_set(EXP_LN_SET)
                        seed_y(LAST)
                        nc.scalar.preload_act_table_set(SILU_SET)
                    if p == "d" and not last:
                        hooks(HOOKS_D, s, t + 1, GELU_SET)
                    if p == "c" and last:
                        hooks(HOOKS_C, s, 0, SILU_SET)
                if last and p == "e":
                    return
                q, u = (NEXT[p], 0) if last else (p, t + 1)
                act.wait_ge(f.up, UPS[p] * NB[p] * (t + 1))
                if q == "d":
                    split(nd.h_ok, NC * (u + 1))
                    take_gates(u, last)
                else:
                    split(x_in, 16 * (NT * (PASS[q] - 1) + u + 1))
                if q in "de":
                    rows_of_gates(q, u)

            for p in "bcde":
                nc.scalar.preload_act_table_set(SILU_SET if UPS[p] == 2 else GELU_SET)
                if p == "b":
                    tile(p, 0, tail=True)
                if p == "d":
                    act.wait_ge(const_in, 4 * 16)
                with act.Fori(1 if p == "b" else 0, LAST) as t:
                    tile(p, t)
                tile(p, LAST, last=True)

        @block.vector
        def _(dve):
            nc.vector.memset(eps_ln, LN_EPS)
            nc.vector.memset(eps_rms, RMS_EPS)
            nc.vector.memset(seed_shift, math.log(SEED_SCALE))
            nc.vector.memset(mean_w[:, :], 1.0 / D).then_inc(ones_ok, 1)
            nc.vector.memset(carry_kv[:, :], 0.0).then_inc(carry_ok, 1)
            nc.vector.memset(carry_w[:, :], W_EPS).then_inc(carry_ok, 1)
            nc.vector.memset(mod_t[:, :, 6 * NC:6 * NC + 1], 1.0)
            nc.vector.memset(mod_t[:, :, 6 * NC + 1:6 * NC + 2], 0.0).then_inc(keep_ok, 1)
            dve.wait_ge(c_exp, 1)
            nc.vector.tensor_scalar(c_e[:, :], c_e[:, :], 1.0, None, ALU.add).then_inc(setup_v, 1)
            dve.wait_ge(setup_v, 1)
            nc.vector.reciprocal(c_e[:, :], c_e[:, :]).then_inc(setup_v, 1)
            dve.wait_ge(setup_v, 2)
            nc.vector.tensor_tensor(c_t[:, :], c_t[:, :], c_e[:, :], ALU.mult).then_inc(c_silu, 1)
            dve.wait_ge(keep_ok, 1)
            nc.vector.memset(mod_t[:, T_SEQ - 1, 6 * NC:6 * NC + 1], 0.0)
            nc.vector.memset(mod_t[:, T_SEQ - 1, 6 * NC + 1:6 * NC + 2], W_EPS)

            def modulation(half):
                n = 3 * NC * NB_SEQ
                part = mod_raw[:, half * n:(half + 1) * n]
                scale, gain = [part[:, k * n // 3:(k + 1) * n // 3] for k in (1, 2)]
                dve.wait_ge(mod_tr, 3 * half + 3)
                nc.vector.tensor_copy(part, b_qk[:, half * n:(half + 1) * n]).then_inc(mod_cp, 1)
                dve.wait_ge(mod_cp, half + 1)
                k = 2 + 5 * half
                sign = mod_tmp[:, half * n // 3:(half + 1) * n // 3]
                nc.vector.tensor_scalar(scale, scale, -0.5, -0.5, ALU.mult, ALU.add).then_inc(setup_v, 1)
                nc.vector.tensor_scalar(sign, gain, 0.0, 2.0, ALU.is_ge, ALU.mult).then_inc(setup_v, 1)
                dve.wait_ge(setup_v, k + 2)
                nc.vector.tensor_scalar(sign, sign, 1.0, None, ALU.subtract).then_inc(setup_v, 1)
                dve.wait_ge(setup_v, k + 3)
                nc.vector.tensor_tensor(gain, gain, sign, ALU.mult).then_inc(setup_v, 1)
                dve.wait_ge(setup_v, k + 4)
                nc.vector.scalar_tensor_tensor(out=gain, in0=gain, scalar=0.25, in1=sign, op0=ALU.max,
                                               op1=ALU.mult).then_inc(setup_v, 1)
                dve.wait_ge(setup_v, k + 5)
                by_seq = part.rearrange("p (k b o) -> p b o k", b=NB_SEQ, o=1)
                for b in range(NB_SEQ):
                    ins = nc.vector.tensor_copy(
                        mod_t[:, b * T_SEQ:(b + 1) * T_SEQ, half * 3 * NC:(half + 1) * 3 * NC],
                        by_seq[:, b].broadcast_to([P, T_SEQ, 3 * NC]))
                ins.then_inc(mod_ok, 1)

            def newton(y, f, src, eps, chain, n, done):
                nc.vector.scalar_tensor_tensor(out=f[:, :], in0=src[:, :], scalar=eps, in1=f[:, :],
                                               op0=ALU.add, op1=ALU.mult).then_inc(chain, 1)
                dve.wait_ge(chain, n + 1)
                dve.sem_inc(settled)
                nc.vector.scalar_tensor_tensor(out=y[:, :], in0=f[:, :], scalar=3.0, in1=y[:, :],
                                               op0=ALU.subtract, op1=ALU.mult).then_inc(done, 1)

            def split(g, scale=1.0):
                for m in range(NC):
                    dve.wait_ge(xh_ok, g + m + 1)
                    dve.sem_inc(settled)
                    if scale == 1.0:
                        nc.vector.tensor_tensor(ch(x_lo, m), ch(x_t, m), ch(x_hi, m).bitcast(F32),
                                                ALU.subtract).then_inc(xl_ok, 1)
                    else:
                        nc.vector.scalar_tensor_tensor(out=ch(x_lo, m), in0=ch(x_t, m), scalar=scale,
                                                       in1=ch(x_hi, m).bitcast(F32), op0=ALU.mult,
                                                       op1=ALU.subtract).then_inc(xl_ok, 1)

            def norm_d(n, src, u):
                dve.wait_ge(n.mean_mm, u + 1)
                dve.sem_inc(settled)
                nc.vector.tensor_tensor(rows(src), rows(src), over_chunks(b_x), ALU.subtract).then_inc(n.d_ok, 1)

            def norm_rstd(n, u):
                dve.wait_ge(n.seed_ok, u + 1)
                dve.sem_inc(settled)
                newton(rs_x, nt_x, b_x, LN_EPS, n.newton, u, n.rstd_ok)

            def norm_dr(n, src, u):
                dve.wait_ge(n.rstd_ok, u + 1)
                dve.sem_inc(settled)
                nc.vector.tensor_tensor(rows(x_t), rows(src), over_chunks(rs_x), ALU.mult).then_inc(n.dr_ok, 1)

            def norm_residual(u):
                dve.wait_ge(r_in, 16 * (u + 1))
                dve.sem_inc(settled)
                for m in range(NC):
                    dve.wait_ge(na.h_ok, NC * u + m + 1)
                    dve.sem_inc(settled)
                    nc.vector.scalar_tensor_tensor(out=ch(r_t, m), in0=ch(x_t, m), scalar=vec(u, GA, m),
                                                   in1=ch(r_t, m), op0=ALU.mult, op1=ALU.add).then_inc(na.r_ok, 1)

            def norm_n(u):
                dve.wait_ge(na.seedr_ok, u + 1)
                dve.sem_inc(settled)
                newton(rs_x, nt_x, b_x, RMS_EPS, na.newtonr, u, na.rrms_ok)
                dve.wait_ge(na.rrms_ok, u + 1)
                dve.sem_inc(settled)
                dve.wait_ge(na.r_ok, NC * (u + 1))
                dve.sem_inc(settled)
                nc.vector.tensor_tensor(rows(x_t), rows(x_t), over_chunks(rs_x), ALU.mult).then_inc(na.n_ok, 1)

            dve.wait_ge(xa_in, 16)
            norm_d(na, x_a, 0)
            norm_rstd(na, 0)
            norm_dr(na, x_a, 0)
            modulation(0)
            norm_residual(0)
            norm_n(0)
            split(0, -0.5)
            modulation(1)
            norm_d(na, x_a, 1)
            dve.wait_ge(mod_ok, 2)

            def scans(t, first=False):
                if first:
                    dve.wait_ge(carry_ok, 2)
                else:
                    dve.wait_ge(y_st, 16 * t)
                    dve.sem_inc(settled)
                    dve.wait_ge(a.carry, 2 * t)
                    dve.sem_inc(settled)
                for m in range(NC):
                    dve.wait_ge(a.wv_ok, NC * t + m + 1)
                    dve.sem_inc(settled)
                    nc.vector.tensor_tensor_scan(ch(kv_t, m), ch(wv_t, m), ch(wv_t, m), carry_kv[:, m:m + 1],
                                                 ALU.add, ALU.bypass).then_inc(a.scan_ok, 1)
                    nc.vector.tensor_tensor_scan(ch(wc_t, m), ch(k_t, m), ch(k_t, m), carry_w[:, m:m + 1],
                                                 ALU.add, ALU.bypass).then_inc(a.scan_ok, 1)
                dve.wait_ge(a.scan_ok, 2 * NC * (t + 1))
                dve.sem_inc(settled)
                keep = mod_t[:, t, 6 * NC:6 * NC + 1]
                fresh = mod_t[:, t, 6 * NC + 1:6 * NC + 2]
                nc.vector.tensor_scalar(carry_kv[:, :], rows(kv_t)[:, :, TT - 1], keep, None,
                                        ALU.mult).then_inc(a.carry, 1)
                nc.vector.tensor_scalar(carry_w[:, :], rows(wc_t)[:, :, TT - 1], keep, fresh,
                                        ALU.mult, ALU.add).then_inc(a.carry, 1)

            def denominator(t):
                dve.wait_ge(a.carry, 2 * t + 2)
                dve.sem_inc(settled)
                dve.wait_ge(a.e_ok, t + 1)
                dve.sem_inc(settled)
                nc.vector.scalar_tensor_tensor(out=wc_t[:, :], in0=q_t[:, :], scalar=1.0, in1=wc_t[:, :],
                                               op0=ALU.add, op1=ALU.mult).then_inc(a.den_ok, 1)

            def tail_0(t):
                dve.wait_ge(a.seed_y, t + 1)
                dve.sem_inc(settled)
                nc.vector.tensor_tensor(kv_t[:, :], kv_t[:, :], q_t[:, :], ALU.mult)
                nc.vector.tensor_tensor(wc_t[:, :], wc_t[:, :], q_t[:, :], ALU.mult).then_inc(a.y0_ok, 1)

            def tail_1(t):
                dve.wait_ge(a.y0_ok, t + 1)
                dve.sem_inc(settled)
                nc.vector.scalar_tensor_tensor(out=kv_t[:, :], in0=wc_t[:, :], scalar=2.0, in1=kv_t[:, :],
                                               op0=ALU.subtract, op1=ALU.mult, reverse0=True).then_inc(a.y_ok, 1)

            def tile_a(t, stage1=True, stage2=True, tail=True):
                u = t + 1
                if tail:
                    scans(t - 1, first=isinstance(t, int) and t == 1)
                if stage2:
                    norm_rstd(na, u)
                    dve.wait_ge(xl_ok, NC * u)
                    dve.sem_inc(settled)
                    norm_dr(na, x_a, u)
                if tail:
                    denominator(t - 1)
                if stage2:
                    norm_residual(u)
                if tail:
                    tail_0(t - 1)
                dve.wait_ge(a.seed_k, t + 1)
                dve.sem_inc(settled)
                newton(rs_qk, nt_qk, b_qk, RMS_EPS, a.newton, 2 * t, a.rk_ok)
                if stage2:
                    norm_n(u)
                if stage1:
                    norm_d(na, x_a, u + 1)
                if tail:
                    tail_1(t - 1)
                if stage2:
                    split(NC * u, -0.5)
                dve.wait_ge(a.seed_q, t + 1)
                dve.sem_inc(settled)
                newton(rs_qk, nt_qk, b_qk, RMS_EPS, a.newton, 2 * t + 1, a.rq_ok)
                dve.wait_ge(a.w_ok, t + 1)
                dve.sem_inc(settled)
                for m in range(NC):
                    if m < NC - 1:
                        dve.wait_ge(a.mm, (NQKV - 1) * t + 2 * NC + m + 1)
                    else:
                        dve.wait_ge(a.x_used, NC * (t + 1))
                    dve.sem_inc(settled)
                    nc.vector.tensor_tensor(ch(wv_t, m), ch(k_t, m), bank[(2 * NC + m) % 6][:, :],
                                            ALU.mult).then_inc(a.wv_ok, 1)

            tile_a(0, tail=False)
            tile_a(1)
            with dve.Fori(2, LAST - 1) as t:
                tile_a(t)
            tile_a(LAST - 1, stage1=False)
            tile_a(LAST, stage1=False, stage2=False)
            split(NC * NT)
            scans(LAST)
            denominator(LAST)

            GCH = 12

            def gating(u):
                n = [GCH * u]

                def then(ins):
                    n[0] = n[0] + 1
                    ins.then_inc(nd.gate_chain, 1)
                    dve.wait_ge(nd.gate_chain, n[0])
                    dve.sem_inc(settled)

                def first_max(onehot, src, top):
                    then(nc.vector.reduce_max(top[:, :], src[:, :, :], axis=AX_X))
                    then(nc.vector.tensor_tensor(eq[:, :, :], src[:, :, :], wide(top), ALU.is_equal))
                    then(nc.vector.tensor_tensor(eq[:, :, :], eq[:, :, :], ranks, ALU.mult))
                    then(nc.vector.reduce_max(fst[:, :], eq[:, :, :], axis=AX_X))
                    then(nc.vector.tensor_tensor(onehot[:, :, :], eq[:, :, :], wide(fst), ALU.is_equal))

                dve.wait_ge(nd.logit_mm, u + 1)
                dve.sem_inc(settled)
                then(nc.vector.tensor_copy(lg[:, :, :], b_x[:, 0:NSUB * E].rearrange("p (s e) -> p s e", s=NSUB)))
                first_max(top1, lg, m1)
                then(nc.vector.scalar_tensor_tensor(out=lg2[:, :, :], in0=top1[:, :, :], scalar=-3.0e38,
                                                    in1=lg[:, :, :], op0=ALU.mult, op1=ALU.add))
                first_max(top2, lg2, m2)
                nc.vector.tensor_tensor(m2[:, :], m2[:, :], m1[:, :], ALU.subtract).then_inc(nd.top_ok, 1)

            def gates(u):
                k = [0]

                def then(ins):
                    k[0] += 1
                    ins.then_inc(gate_fin, 1)
                    dve.wait_ge(gate_fin, 7 * u + k[0])
                    dve.sem_inc(settled)

                dve.wait_ge(nd.e_ok, u + 1)
                dve.sem_inc(settled)
                then(nc.vector.tensor_scalar(g1[:, :], g2[:, :], 1.0, None, ALU.add))
                then(nc.vector.reciprocal(g1[:, :], g1[:, :]))
                then(nc.vector.tensor_tensor(g2[:, :], g2[:, :], g1[:, :], ALU.mult))
                then(nc.vector.tensor_tensor(top1[:, :, :], top1[:, :, :], wide(g1), ALU.mult))
                then(nc.vector.tensor_tensor(top2[:, :, :], top2[:, :, :], wide(g2), ALU.mult))
                then(nc.vector.tensor_tensor(top1[:, :, :], top1[:, :, :], top2[:, :, :], ALU.add))
                then(nc.vector.tensor_copy(gates_tok[:, :, 0:E].bitcast(F32R), top1[:, :, :]))
                nc.vector.tensor_tensor(gates_tok[:, :, E:2 * E], top1[:, :, :], gates_tok[:, :, 0:E],
                                        ALU.subtract).then_inc(nd.gt_ok, 1)

            def wide(t):
                return t[:, :].rearrange("p (s o) -> p s o", o=1).broadcast_to([P, NSUB, E])

            ranks = rank_t[:, :].rearrange("p (o e) -> p o e", o=1).broadcast_to([P, NSUB, E])

            def hooks(h, s, u):
                if s == h["mean"]:
                    norm_d(nd, x_t, u)
                if s == h["var"]:
                    norm_rstd(nd, u)
                    norm_dr(nd, x_t, u)
                if s == h["logit"]:
                    gating(u)
                if s == h["e"]:
                    gates(u)

            def block_(p, t, s):
                f, nb = ffn[p], NB[p]
                routed = s < N_ROUTED[p]
                if UPS[p] == 2:
                    dve.wait_ge(f.up, 2 * (nb * t + s) + 2)
                    dve.sem_inc(settled)
                dve.wait_ge(f.act_ok, nb * t + s + 1)
                dve.sem_inc(settled)
                if UPS[p] == 2:
                    other = bank[4 + (2 * s + 1) % 3][:, :]
                elif routed:
                    per_tile = N_ROUTED[p] // 2 + (1 if p == "e" else 0)
                    dve.wait_ge(f.gb, per_tile * t + s // 2 + 1 + (1 if p == "e" and s >= 4 else 0))
                    dve.sem_inc(settled)
                    other = bank[6][:, :]
                if UPS[p] == 2 or routed:
                    nc.vector.tensor_tensor(s_t[:, s % 2, :], act_t[:, s % 2, :], other, ALU.mult).then_inc(f.s_ok, 1)
                else:
                    nc.vector.tensor_copy(s_t[:, s % 2, :], act_t[:, s % 2, :]).then_inc(f.s_ok, 1)
                dve.wait_ge(f.sh_ok, nb * t + s + 1)
                dve.sem_inc(settled)
                nc.vector.tensor_tensor(s_lo[:, s % 3, :], s_t[:, s % 2, :], s_hi[:, s % 3, :].bitcast(F32),
                                        ALU.subtract).then_inc(f.sl_ok, 1)

            def tile(p, t, last=False, tail=False):
                f, nb = ffn[p], NB[p]
                for s in range(nb):
                    block_(p, t, s)
                    if tail and s == 1:
                        tail_0(LAST)
                    if tail and s == 2:
                        tail_1(LAST)
                    if p == "d" and not last:
                        hooks(HOOKS_D, s, t + 1)
                    if p == "c" and last:
                        hooks(HOOKS_C, s, 0)
                if not (last and p == "e"):
                    q, u = (NEXT[p], 0) if last else (p, t + 1)
                    split(NC * (NT * PASS[q] + u))
                dve.wait_ge(f.dn, nb * (t + 1))
                dve.sem_inc(settled)
                dve.wait_ge(r_in, 16 * (NT * PASS[p] + t + 1))
                dve.sem_inc(settled)
                for m in range(NC):
                    nc.vector.scalar_tensor_tensor(out=ch(r_t, m), in0=bank[m][:, :], scalar=vec(t, GAIN[p], m),
                                                   in1=ch(r_t, m), op0=ALU.mult, op1=ALU.add).then_inc(f.ev_ok, 1)

            for p in "bcde":
                if p == "b":
                    tile(p, 0, tail=True)
                    dve.wait_ge(y_st, 16 * NT)
                    dve.wait_ge(const_in, 4 * 16)
                    nc.vector.memset(gates_tok[:, :, :], 0.0).then_inc(ones_ok, 1)
                    dve.wait_ge(ones_ok, 2)
                    nc.vector.memset(gates_tok[:, :, 2 * E:NG], 1.0).then_inc(ones_ok, 1)
                with dve.Fori(1 if p == "b" else 0, LAST) as t:
                    tile(p, t)
                tile(p, LAST, last=True)


def kernel(**inputs):
    import concourse.bacc as bacc
    import numpy as np
    from concourse.bass_utils import run_bass_kernel_spmd

    x = np.ascontiguousarray(inputs["L0_attn_x"])
    B, S, D = x.shape
    nc_, nt = D // P, B * S // TT
    E, _, H = inputs["L0_ffn_w1"].shape

    def blocks(w, rows_, cols):
        return np.asarray(w).reshape(rows_ // P, P, cols // P, P).transpose(2, 0, 1, 3)

    w_qkv = blocks(np.asarray(inputs["L0_attn_w_qkv"]).T, D, 3 * D)
    w_qkv = np.concatenate([w_qkv[nc_:2 * nc_], w_qkv[0:nc_], w_qkv[2 * nc_:]])
    w_qkv = w_qkv.reshape(nc_, 3 * nc_, P, P).transpose(0, 2, 1, 3).reshape(nc_, P, 3 * nc_ * P)
    swi = np.asarray(inputs["L0_attn_w_swiglu"])
    F = swi.shape[0] // 2
    up = blocks(swi.T, D, 2 * F)
    down = np.asarray(inputs["L0_attn_w_out"]).T.reshape(F // P, P, nc_, P).transpose(0, 2, 1, 3)
    w_swi = np.concatenate([up[F // P:], up[:F // P], down], axis=1)
    w_swi = w_swi.transpose(0, 2, 1, 3).reshape(F // P, P, 3 * nc_ * P)
    w1 = np.concatenate([blocks(w, D, H) for w in np.asarray(inputs["L0_ffn_w1"])]
                        + [blocks(inputs["L0_ffn_shared_w1"], D, D)])
    w2 = np.concatenate([np.asarray(inputs["L0_ffn_w2"]).reshape(E * H, D), np.asarray(inputs["L0_ffn_shared_w2"])])
    w2 = w2.reshape(-1, P, nc_, P).transpose(0, 2, 1, 3)
    w_moe = np.concatenate([w1, w2], axis=1).transpose(0, 2, 1, 3).reshape(-1, P, 2 * nc_ * P)
    b1 = np.concatenate([np.asarray(inputs["L0_ffn_b1"]).reshape(-1), np.asarray(inputs["L0_ffn_shared_b1"])])
    b2 = np.asarray(inputs["L0_ffn_b2"])
    b2 = np.concatenate([b2, b2, np.asarray(inputs["L0_ffn_shared_b2"])[None]])
    c = np.asarray(inputs["L0_c"]).reshape(B, nc_, P).transpose(2, 1, 0).reshape(P, nc_ * B)
    wmod = np.asarray(inputs["L0_wmod"]).reshape(nc_, P, 6, D).transpose(2, 1, 0, 3).reshape(6, P, nc_ * D)
    gate_w = np.asarray(inputs["L0_ffn_gate_w"]).reshape(nc_, P, E).transpose(1, 0, 2).reshape(P, nc_ * E)
    arrays = {
        "x": x.reshape(nt, TT, nc_, P).transpose(0, 3, 2, 1).reshape(nt, P, nc_ * TT),
        "c": c, "wmod": wmod, "w_qkv": w_qkv, "w_swi": w_swi, "w_moe": w_moe,
        "b1": b1.reshape(-1, P).T, "b2": b2, "gate_w": gate_w,
        "select": np.repeat(np.concatenate([np.eye(E), np.eye(E)]), P, axis=1).astype(np.float32),
        "ident": np.eye(P, dtype=np.float32),
        "rank": np.tile(np.arange(E, 0, -1, dtype=np.float32), (P, 1)),
    }
    arrays = {k: np.ascontiguousarray(v) for k, v in arrays.items()}
    nc = bacc.Bacc("TRN2", target_bir_lowering=False, num_devices=1)
    args = [nc.dram_tensor(k, v.shape, mybir.dt.from_np(v.dtype), kind="ExternalInput").ap()
            for k, v in arrays.items()]
    out = nc.dram_tensor("out", (nt, P, nc_ * TT), F32, kind="ExternalOutput").ap()
    build(nc, *args, out)
    r = run_bass_kernel_spmd(nc, [arrays], core_ids=[0])
    got = np.asarray(r.results[0]["out"]).reshape(nt, P, nc_, TT).transpose(0, 3, 2, 1)
    return np.ascontiguousarray(got).reshape(B, S, D)
```

```python
from collections import namedtuple
from contextlib import ExitStack
import math

import concourse.bass as bass
from concourse import mybir

F32 = mybir.dt.float32
F32R = mybir.dt.float32r
ALU = mybir.AluOpType
ACT = mybir.ActivationFunctionType
AX_X = mybir.AxisListType.X

P = 128
TT = 512
LN_EPS = 1e-05
W_EPS = 1e-06
RMS_EPS = 1.1920929e-07
SEED_SCALE = 2.0 ** -16
EXP_LN_SET = "natural_log_exp_and_others"
SILU_SET = "silu_and_others"
GELU_SET = "gelu_and_others"
SA, CA, GA, SB, CB, GB = range(6)


def build(nc, x, c, wmod, w_qkv, w_swi, w_moe, b1, b2, gate_w, select, ident, rank, out):
    NT = x.shape[0]
    D = x.shape[2] // TT * P
    NC = D // P
    NB_SEQ = c.shape[1] // NC
    T_SEQ = NT // NB_SEQ
    E = gate_w.shape[1] // NC
    ONES = 2 * E
    AGAIN = 32
    NG = AGAIN + ONES + 1
    NQKV = 3 * NC
    ROUTED = w_moe.shape[0] - NC
    SWI_W = w_swi.shape[2]
    MOE_W = w_moe.shape[2]
    QKV_W = NC * P
    CHW = NC * TT
    W_COLS = 8 * SWI_W
    NSUB = TT // P
    LAST = NT - 1
    NB_SWI = w_swi.shape[0] // 2
    NB_MOE = w_moe.shape[0] // 2
    assert NC == 4 and NB_SEQ == 2 and NB_SWI * SWI_W == W_COLS and NB_MOE * MOE_W <= W_COLS

    QKV_PIECES = w_qkv.shape[0]
    swi_col = [(j + NB_SWI // 2) % NB_SWI * SWI_W for j in range(NB_SWI)]
    moe_col = [(swi_col[0] + j * MOE_W) % W_COLS for j in range(NB_MOE)]
    pieces = [(w_qkv[i], i * SWI_W, SWI_W) for i in range(QKV_PIECES)]
    B0 = len(pieces)
    pieces += [(w_swi[j], swi_col[j], SWI_W) for j in range(NB_SWI)]
    C0 = len(pieces)
    pieces += [(w_swi[NB_SWI + j], swi_col[j], SWI_W) for j in range(NB_SWI)]
    D0 = len(pieces)
    pieces += [(w_moe[j], moe_col[j], MOE_W) for j in range(NB_MOE)]
    E0 = len(pieces)
    pieces += [(w_moe[NB_MOE + j], moe_col[j], MOE_W) for j in range(NB_MOE)]

    y_dram = nc.dram_tensor("y_scratch", (NT, P, CHW), F32, kind="Internal").ap()
    ra_dram = nc.dram_tensor("residual_a", (NT, P, CHW), F32, kind="Internal").ap()
    rb_dram = nc.dram_tensor("residual_b", (NT, P, CHW), F32, kind="Internal").ap()
    g_dram = nc.dram_tensor("gate_scratch", (NT, NG, TT), F32, kind="Internal").ap()

    ctx = ExitStack()
    with ctx:
        def sb(name, shape, dt=F32):
            return ctx.enter_context(nc.sbuf_tensor(name, shape, dt))

        def sem(name):
            return ctx.enter_context(nc.semaphore(name))

        def sems(suffix, names):
            return namedtuple("Sems", names)(*[sem(f"{n}_{suffix}") for n in names.split()])

        w_hi = sb("w_hi", [P, W_COLS], F32R)
        w_lo = sb("w_lo", [P, W_COLS], F32R)
        raw = [sb(f"raw{i}", [P, SWI_W]) for i in range(2)]
        x_t = sb("x_t", [P, CHW])
        r_t = sb("r_t", [P, CHW])
        sq_t = sb("sq_t", [P, CHW])
        sum_x = sb("sum_x", [P, TT])
        sum_qk = sb("sum_qk", [P, TT])
        rs_x = sb("rs_x", [P, TT])
        nt_x = sb("nt_x", [P, TT])
        rs_qk = sb("rs_qk", [P, TT])
        nt_qk = sum_qk
        x_hi = sb("x_hi", [P, CHW], F32R)
        x_lo = sb("x_lo", [P, CHW], F32R)
        mod_t = sb("mod_t", [P, NT, 6 * NC + 2])
        mod_raw = sb("mod_raw", [P, 6 * NC * NB_SEQ])
        mod_tmp = sb("mod_tmp", [P, 2 * NC * NB_SEQ])
        c_t = sb("c_t", [P, NC * NB_SEQ])
        c_e = sb("c_e", [P, NC * NB_SEQ])
        id2 = sb("id2", [NB_SEQ, NB_SEQ])
        mean_w = sb("mean_w", [P, P])
        carry_kv = sb("carry_kv", [P, NC])
        carry_w = sb("carry_w", [P, NC])
        eps_t = sb("eps_t", [P, 3])
        eps_ln, eps_rms, seed_shift = eps_t[:, 0:1], eps_t[:, 1:2], eps_t[:, 2:3]

        with ExitStack() as only_a:
            def sa_(name):
                return only_a.enter_context(nc.sbuf_tensor(name, [P, CHW], F32))
            x_a = sa_("x_a")
            k_t = sa_("k_t")
            wv_t = sa_("wv_t")
            q_t = sa_("q_t")
            kv_t = sa_("kv_t")
            wc_t = sa_("wc_t")
        act_t = sb("act_t", [P, 2, TT])
        s_t = sb("s_t", [P, 2, TT])
        s_hi = sb("s_hi", [P, 3, TT], F32R)
        s_lo = sb("s_lo", [P, 3, TT], F32R)
        ident_t = sb("ident_t", [P, P])
        b1_t = sb("b1_t", [P, w_moe.shape[0]])
        gw_t = sb("gw_t", [P, NC * E])
        rank_t = sb("rank_t", [P, E])
        g_next = sb("g_next", [NG, TT])
        g_rows = sb("g_rows", [NG, TT], F32R)
        sel_raw = sb("sel_raw", [2 * E, E * P])
        sel_t = sb("sel_t", [2 * E, E * P], F32R)
        b2_raw = sb("b2_raw", [NG, D])
        b2_parts = sb("b2_parts", [NG, D], F32R)
        gates_tok = sb("gates_tok", [P, NSUB, P])
        lg_rows = sb("lg_rows", [E, TT])
        lg = sb("lg", [P, NSUB, E])
        eq = sb("eq", [P, NSUB, E])
        top1 = sb("top1", [P, NSUB, E])
        lg2 = sb("lg2", [P, NSUB, E])
        top2 = sb("top2", [P, NSUB, E])
        m1 = sb("m1", [P, NSUB])
        m2 = sb("m2", [P, NSUB])
        fst = sb("fst", [P, NSUB])
        g1 = sb("g1", [P, NSUB])
        g2 = sb("g2", [P, NSUB])
        bank = [ctx.enter_context(nc.psum_tensor(f"bank{i}", [P, TT], F32)) for i in range(8)]
        b_qk, b_x = bank[6], bank[7]

        const_in, c_in, sel_in = sem("const_in"), sem("c_in"), sem("sel_in")
        wmod_in = [sem(f"wmod_in{v}") for v in range(6)]
        raw_in = [sem("raw_in0"), sem("raw_in1")]
        w_hi_ok, w_ok = sem("w_hi_ok"), sem("w_ok")
        ones_ok, carry_ok, keep_ok = sem("ones_ok"), sem("carry_ok"), sem("keep_ok")
        c_exp, c_silu, id2_in = sem("c_exp"), sem("c_silu"), sem("id2_in")
        mod_mm, mod_row, mod_tr, mod_cp, mod_ok = [sem(n) for n in ("mod_mm", "mod_row", "mod_tr", "mod_cp", "mod_ok")]
        xa_in, x_in, r_in, r_st = sem("xa_in"), sem("x_in"), sem("r_in"), sem("r_st")
        xh_ok, xl_ok = sem("xh_ok"), sem("xl_ok")
        y_st, h_st, g_st, out_st = sem("y_st"), sem("h_st"), sem("g_st"), sem("out_st")
        g_in, sel_ok = sem("g_in"), sem("sel_ok")
        settled = sem("settled")
        setup_v = sem("setup_v")
        LN = "sum0 mean_mm d_ok dsq_ok sum1 var_mm ln_ok seed_ok newton rstd_ok dr_ok h_ok half"
        na = sems("norm_a", LN + " hsq_ok sum2 rms_mm rrms_ok n_ok r_ok halfr lnr_ok seedr_ok newtonr")
        nd = sems("norm_d", LN + " logit_mm rows_ok lt_mm top_ok e_ok gate_chain gt_ok tr_mm gp_ok")
        a = sems("qkv", "mm x_used kq_ev ksum k_mm ln_k seed_k newton rk_ok kn_ok w_ok qsum q_mm ln_q seed_q rq_ok qn_ok "
                      "e_ok wv_ok scan_ok carry den_ok ln_y seed_y y0_ok y_ok halfqk")
        ffn = {p: sems(p, "up act_ok s_ok sh_ok sl_ok dn ev_ok gb") for p in "bcde"}
        g_cp, gate_fin = sem("g_cp"), sem("gate_fin")
        final_dn = sem("final_dn")

        PASS = {"a": 0, "b": 1, "c": 2, "d": 3, "e": 4}
        NB = {"b": NB_SWI, "c": NB_SWI, "d": NB_MOE, "e": NB_MOE}
        W0 = {"b": B0, "c": C0, "d": D0, "e": E0}
        UPS = {"b": 2, "c": 2, "d": 1, "e": 1}
        GAIN = {"b": GA, "c": GA, "d": GB, "e": GB}
        NEXT = {"a": "b", "b": "c", "c": "d", "d": "e"}
        N_ROUTED = {"b": 0, "c": 0, "d": NB_MOE, "e": ROUTED - NB_MOE}
        HOOKS_C = dict(mean=1, sq=1, var=3, h=4, logit=5, top=6, e=7, tr=9)
        HOOKS_D = dict(mean=3, sq=3, var=5, h=6, logit=7, top=8, e=9, tr=11)

        def ch(t, m):
            return t[:, m * TT:(m + 1) * TT]

        def rows(t):
            return t[:, :].rearrange("p (c n) -> p c n", c=NC)

        def over_chunks(t):
            return t[:, :].rearrange("p (o n) -> p o n", o=1).broadcast_to([P, NC, TT])

        def sums(n, u):
            return u if n is na else u + 1

        def vec(t, v, m):
            return mod_t[:, t, v * NC + m:v * NC + m + 1]

        halves = [slice(0, CHW // 2), slice(CHW // 2, CHW)]

        wmod_bufs = [k_t, q_t, wv_t, kv_t, wc_t, k_t]

        block = ctx.enter_context(nc.Block())

        @block.sync
        def _(sp):
            def piece(i):
                if i >= 2:
                    sp.wait_ge(w_ok, i - 1)
                src, _, n = pieces[i]
                sp.dma_start(raw[i % 2][:, 0:n], src).then_inc(raw_in[i % 2], 16)

            def load_x(src, t):
                sp.dma_start(x_t[:, :], src[t]).then_inc(x_in, 16)

            def load_r(src, t):
                sp.dma_start(r_t[:, :], src[t]).then_inc(r_in, 16)

            def load_xa(t):
                sp.dma_start(x_a[:, :], x[t]).then_inc(xa_in, 16)

            sp.dma_start(c_t[:, :], c).then_inc(c_in, 16)
            load_xa(0)
            sp.dma_start(id2[:, :], ident[0:NB_SEQ, 0:NB_SEQ]).then_inc(id2_in, 16)
            for v in range(3):
                sp.dma_start(wmod_bufs[v][:, :], wmod[v]).then_inc(wmod_in[v], 16)
            piece(0)
            piece(1)
            for v in (3, 4):
                sp.dma_start(wmod_bufs[v][:, :], wmod[v]).then_inc(wmod_in[v], 16)
            load_r(x, 0)
            sp.wait_ge(mod_tr, 1)
            sp.dma_start(wmod_bufs[5][:, :], wmod[5]).then_inc(wmod_in[5], 16)
            piece(2)
            sp.wait_ge(na.dr_ok, NC)
            load_xa(1)
            piece(3)
            sp.wait_ge(na.r_ok, NC)
            sp.dma_start(ra_dram[0], r_t[:, :]).then_inc(r_st, 16)
            sp.wait_ge(r_st, 16)
            load_r(x, 1)
            piece(4)
            piece(5)

            def tile_a(t, stage1=True, stage2=True, tail=True):
                u = t + 1
                if stage1:
                    sp.wait_ge(na.dr_ok, NC * (u + 1))
                    sp.sem_inc(settled)
                    load_xa(u + 1)
                if stage2:
                    sp.wait_ge(na.r_ok, NC * (u + 1))
                    sp.sem_inc(settled)
                    sp.dma_start(ra_dram[u], r_t[:, :]).then_inc(r_st, 16)
                    sp.wait_ge(r_st, 16 * (u + 1))
                    sp.sem_inc(settled)
                    if stage1:
                        load_r(x, u + 1)
                    else:
                        load_r(ra_dram, 0)
                if tail:
                    sp.wait_ge(a.y_ok, t)
                    sp.sem_inc(settled)
                    sp.dma_start(y_dram[t - 1], kv_t[:, :]).then_inc(y_st, 16)

            tile_a(0, tail=False)
            with sp.Fori(1, LAST - 1) as t:
                tile_a(t)
            piece(6)
            tile_a(LAST - 1, stage1=False)
            piece(7)
            sp.wait_ge(xl_ok, NC * NT)
            sp.wait_ge(y_st, 16)
            load_x(y_dram, 0)
            tile_a(LAST, stage1=False, stage2=False)
            for i in range(8, C0):
                piece(i)
            sp.wait_ge(a.y_ok, NT)
            sp.dma_start(y_dram[LAST], kv_t[:, :]).then_inc(y_st, 16)
            sp.wait_ge(y_st, 16 * NT)
            sp.dma_start(sel_raw[:, :], select).then_inc(sel_in, 16)
            sp.dma_start(b2_raw[:, :], b2).then_inc(sel_in, 16)
            for dst, src in ((ident_t, ident), (b1_t, b1), (gw_t, gate_w), (rank_t, rank)):
                sp.dma_start(dst[:, :], src).then_inc(const_in, 16)

            X_SRC = {"b": y_dram, "c": y_dram, "d": ra_dram, "e": y_dram}
            R_SRC = {"b": ra_dram, "c": rb_dram, "d": ra_dram, "e": rb_dram}
            R_DST = {"b": rb_dram, "c": ra_dram, "d": rb_dram, "e": out}

            def next_x(p, t):
                sp.wait_ge(xl_ok, NC * (NT * PASS[p] + t))
                if p == "b":
                    sp.sem_inc(settled)
                    sp.wait_ge(y_st, 16 * (t + 1))
                if p == "d":
                    sp.sem_inc(settled)
                    sp.wait_ge(r_st, 16 * (2 * NT + t + 1))
                    sp.sem_inc(settled)
                    sp.wait_ge(h_st, 16 * t)
                if p == "e":
                    sp.sem_inc(settled)
                    sp.wait_ge(h_st, 16 * NT)
                    sp.wait_ge(g_cp, NT + t)
                    sp.sem_inc(settled)
                    sp.wait_ge(g_st, 16 * NT)
                sp.sem_inc(settled)
                load_x(X_SRC[p], t)
                if p == "e":
                    sp.dma_start(g_next[:, :], g_dram[t]).then_inc(g_in, 16)

            def store_h(t):
                sp.wait_ge(nd.h_ok, NC * (t + 1))
                sp.sem_inc(settled)
                sp.dma_start(y_dram[t], x_t[:, :]).then_inc(h_st, 16)
                sp.wait_ge(nd.gp_ok, t + 1)
                sp.sem_inc(settled)
                sp.dma_start(g_dram[t], g_next[:, :]).then_inc(g_st, 16)

            def tile(p, t, after_next, last=False):
                if last and p != "e":
                    n0 = W0[NEXT[p]]
                    for i in range(n0, n0 + NB[NEXT[p]]):
                        piece(i)
                if p == "d" and not last:
                    store_h(t + 1)
                if p == "c" and last:
                    store_h(0)
                if after_next:
                    next_x(*after_next)
                if last and p == "e":
                    for m in range(NC):
                        sp.wait_ge(ffn[p].ev_ok, NC * t + m + 1)
                        sp.dma_start(ch(out[t], m), ch(r_t, m)).then_inc(out_st, 16)
                    return
                sp.wait_ge(ffn[p].ev_ok, NC * (t + 1))
                sp.sem_inc(settled)
                if p == "e":
                    sp.dma_start(R_DST[p][t], r_t[:, :]).then_inc(out_st, 16)
                    sp.wait_ge(out_st, 16 * (t + 1))
                else:
                    sp.dma_start(R_DST[p][t], r_t[:, :]).then_inc(r_st, 16)
                    sp.wait_ge(r_st, 16 * (NT * PASS[p] + t + 1))
                sp.sem_inc(settled)
                if not last:
                    load_r(R_SRC[p], t + 1)
                elif p != "e":
                    load_r(R_SRC[NEXT[p]], 0)

            next_x("b", 1)
            for p in "bcde":
                q = NEXT.get(p)
                with sp.Fori(0, LAST - 1) as t:
                    tile(p, t, (p, t + 2))
                tile(p, LAST - 1, q and (q, 0))
                tile(p, LAST, q and (q, 1), last=True)
            for s, n in ((y_st, 16 * NT), (h_st, 16 * NT), (g_st, 16 * NT), (r_st, 4 * 16 * NT),
                         (out_st, 16 * (LAST + NC))):
                sp.wait_ge(s, n)

        @block.gpsimd
        def _(pool):
            def piece(i):
                _, col, n = pieces[i]
                pool.wait_ge(raw_in[i % 2], 16 * (i // 2 + 1))
                src = raw[i % 2][:, 0:n]
                nc.gpsimd.tensor_scalar(w_hi[:, col:col + n], src, 1.0, 1.0, ALU.mult, ALU.mult).then_inc(w_hi_ok, 1)
                pool.wait_ge(w_hi_ok, i + 1)
                nc.gpsimd.tensor_tensor(w_lo[:, col:col + n], src, w_hi[:, col:col + n].bitcast(F32),
                                        ALU.subtract).then_inc(w_ok, 1)

            def chunk_sum(dst, src, ready, before, chain, n, done):
                for m in range(1, NC):
                    if ready is not None:
                        pool.wait_ge(ready, before + m + 1)
                    if m > 1:
                        pool.wait_ge(chain, n + m - 1)
                    ins = nc.gpsimd.tensor_tensor(dst[:, :], ch(src, 0) if m == 1 else dst[:, :], ch(src, m), ALU.add)
                    ins.then_inc(chain if m < NC - 1 else done, 1)

            def sum_x0(n, src, arrived, count, u):
                pool.wait_ge(arrived, count)
                chunk_sum(sum_x, src, None, 0, n.half, 4 * (sums(n, u) - 1), n.sum0)

            def sum_d(n, u):
                chunk_sum(sum_x, sq_t, n.dsq_ok, NC * u, n.half, 4 * (sums(n, u) - 1) + 2, n.sum1)

            def sum_h(u):
                chunk_sum(sum_x, sq_t, na.hsq_ok, NC * u, na.halfr, 2 * (u - 1), na.sum2)

            for i in range(3):
                piece(i)
            sum_x0(na, x_a, xa_in, 32, 1)
            piece(3)
            sum_d(na, 1)

            def sum_k(t):
                chunk_sum(sum_qk, wv_t, a.kq_ev, 2 * NC * t, a.halfqk, 4 * t, a.ksum)

            def norm_k(t):
                pool.wait_ge(a.rk_ok, t + 1)
                nc.gpsimd.tensor_tensor(rows(k_t), rows(k_t), over_chunks(rs_qk), ALU.mult).then_inc(a.kn_ok, 1)

            def sum_q(t, squares):
                pool.wait_ge(a.rk_ok, t + 1)
                chunk_sum(sum_qk, squares, a.kq_ev, 2 * NC * t + NC, a.halfqk, 4 * t + 2, a.qsum)

            def norm_q(t):
                pool.wait_ge(a.rq_ok, t + 1)
                nc.gpsimd.tensor_tensor(rows(q_t), rows(q_t), over_chunks(rs_qk), ALU.mult).then_inc(a.qn_ok, 1)

            def tile_a(t, stage1=True, stage2=True):
                u = t + 1
                sum_k(t)
                if stage2:
                    sum_h(u)
                if stage1:
                    pool.wait_ge(na.rms_mm, u + 1)
                    sum_x0(na, x_a, xa_in, 16 * (u + 2), u + 1)
                norm_k(t)
                sum_q(t, wv_t if stage2 else sq_t)
                if stage1:
                    sum_d(na, u + 1)
                norm_q(t)

            tile_a(0)
            piece(4)
            with pool.Fori(1, LAST - 1) as t:
                tile_a(t)
            tile_a(LAST - 1, stage1=False)
            piece(5)
            tile_a(LAST, stage1=False, stage2=False)
            piece(6)
            piece(7)
            pool.wait_ge(a.x_used, NC * NT)
            for i in range(B0 + NB_SWI // 2, C0):
                piece(i)
            pool.wait_ge(sel_in, 32)
            nc.gpsimd.tensor_scalar(sel_t[:, :], sel_raw[:, :], 1.0, None, ALU.mult).then_inc(sel_ok, 1)
            nc.gpsimd.tensor_scalar(b2_parts[:, :], b2_raw[:, :], 1.0, None, ALU.mult).then_inc(sel_ok, 1)
            pool.wait_ge(sel_ok, 2)
            nc.gpsimd.tensor_tensor(b2_parts[AGAIN:NG, :], b2_raw[AGAIN:NG, :], b2_parts[AGAIN:NG, :].bitcast(F32),
                                    ALU.subtract).then_inc(sel_ok, 1)
            pool.wait_ge(sel_ok, 3)

            def freed_by(col, n, cols, width):
                return max(j for j, k in enumerate(cols) if k < col + n and col < k + width)

            for j in range(NB_SWI):
                pool.wait_ge(ffn["b"].dn, NB_SWI * LAST + j + 1)
                piece(C0 + j)
            for j in range(NB_MOE):
                if j == 0:
                    sum_x0(nd, x_t, x_in, 16 * (2 * NT + 1), 0)
                if j == 1:
                    sum_d(nd, 0)
                pool.wait_ge(ffn["c"].dn, NB_SWI * LAST + freed_by(moe_col[j], MOE_W, swi_col, SWI_W) + 1)
                piece(D0 + j)
            with pool.Fori(0, LAST) as t:
                pool.wait_ge(nd.var_mm, t + 1)
                sum_x0(nd, x_t, x_in, 16 * (2 * NT + t + 2), t + 1)
                sum_d(nd, t + 1)
            for j in range(NB_MOE):
                pool.wait_ge(ffn["d"].dn, NB_MOE * LAST + j + 1)
                piece(E0 + j)

        @block.tensor
        def _(pe):
            def product(dst, rhs_hi, rhs_lo, col, start, stop):
                nc.tensor.matmul(dst, w_hi[:, col:col + P], rhs_hi, start=start, stop=False)
                nc.tensor.matmul(dst, w_hi[:, col:col + P], rhs_lo, start=False, stop=False)
                return nc.tensor.matmul(dst, w_lo[:, col:col + P], rhs_hi, start=False, stop=stop)

            def from_x(dst, col, first_of_tile=None):
                for m in range(NC):
                    if first_of_tile is not None:
                        pe.wait_ge(xl_ok, first_of_tile + m + 1)
                    ins = product(dst, ch(x_hi, m), ch(x_lo, m), col + m * P, m == 0, m == NC - 1)
                return ins

            def mean(dst, src):
                return nc.tensor.matmul(dst[:, :], mean_w[:, :], src[:, :], start=True, stop=True)

            def modulate(v):
                pe.wait_ge(wmod_in[v], 16)
                for k in range(NC):
                    ins = nc.tensor.matmul(bank[v][0:NB_SEQ, :], c_t[:, k * NB_SEQ:(k + 1) * NB_SEQ],
                                           wmod_bufs[v][:, k * D:(k + 1) * D], start=(k == 0), stop=(k == NC - 1))
                ins.then_inc(mod_mm, 1)

            def rows_to_columns(v):
                pe.wait_ge(mod_row, v + 1)
                for m in range(NC):
                    at = (v * NC + m) * NB_SEQ
                    ins = nc.tensor.transpose(b_qk[:, at:at + NB_SEQ], wmod_bufs[v][0:NB_SEQ, m * P:(m + 1) * P],
                                              id2[:, :])
                ins.then_inc(mod_tr, 1)

            def norm_mean(n, u):
                pe.wait_ge(n.sum0, sums(n, u))
                mean(b_x, sum_x).then_inc(n.mean_mm, 1)

            def norm_var(n, u):
                pe.wait_ge(n.sum1, sums(n, u))
                mean(b_x, sum_x).then_inc(n.var_mm, 1)

            def norm_rms(u):
                pe.wait_ge(na.sum2, sums(na, u))
                mean(b_x, sum_x).then_inc(na.rms_mm, 1)

            def mean_of_chunks(dst, src, ready=None):
                for m in range(NC):
                    if ready is not None:
                        pe.wait_ge(ready, m + 1)
                    ins = nc.tensor.matmul(dst[:, :], mean_w[:, :], ch(src, m), start=(m == 0), stop=(m == NC - 1))
                return ins

            pe.wait_ge(ones_ok, 1)
            pe.wait_ge(xa_in, 16)
            mean_of_chunks(bank[5], x_a).then_inc(na.mean_mm, 1)
            pe.wait_ge(c_silu, 1)
            modulate(0)
            mean_of_chunks(b_x, sq_t, na.dsq_ok).then_inc(na.var_mm, 1)
            modulate(1)
            pe.wait_ge(id2_in, 16)
            rows_to_columns(0)
            modulate(2)
            rows_to_columns(1)
            rows_to_columns(2)
            modulate(3)
            mean_of_chunks(b_x, sq_t, na.hsq_ok).then_inc(na.rms_mm, 1)
            modulate(4)
            modulate(5)
            pe.wait_ge(mod_cp, 1)
            for v in (3, 4, 5):
                rows_to_columns(v)
            pe.wait_ge(na.rrms_ok, 1)
            norm_mean(na, 1)

            AFTER_VAR, AFTER_VAR_0, AFTER_K, AFTER_RMS, AFTER_RMS_0 = 0, 2, 5, 6, 7
            AFTER_MEAN, AFTER_Q, AFTER_Q_LAST = 0, 3, 1

            def tile_a(t, first=False, stage1=True, stage2=True):
                u = t + 1
                for o in range(NQKV - 3):
                    pe.wait_ge(w_ok, o // 3 + 1)
                    if o >= 6:
                        pe.wait_ge(a.kq_ev, 2 * NC * t + o - 5)
                    elif o >= 2 and not first:
                        pe.wait_ge(a.wv_ok, NC * (t - 1) + o - 1)
                    from_x(bank[o % 6][:, :], o * QKV_W, NC * t if o == 0 else None).then_inc(a.mm, 1)
                    if o == (AFTER_VAR_0 if first else AFTER_VAR) and stage2:
                        norm_var(na, u)
                    if o == AFTER_K:
                        if first:
                            pe.wait_ge(mod_cp, 2)
                        pe.wait_ge(a.ksum, t + 1)
                        mean(b_qk, sum_qk).then_inc(a.k_mm, 1)
                    if o == (AFTER_RMS_0 if first else AFTER_RMS) and stage2:
                        norm_rms(u)
                pe.wait_ge(w_ok, NC)
                pe.wait_ge(a.kq_ev, 2 * NC * t + NQKV - 6)
                for m in range(NC):
                    for o in range(NQKV - 3, NQKV):
                        ins = product(bank[o % 6][:, :], ch(x_hi, m), ch(x_lo, m), o * QKV_W + m * P,
                                      m == 0, m == NC - 1)
                        if m == NC - 1 and o < NQKV - 1:
                            ins.then_inc(a.mm, 1)
                    ins.then_inc(a.x_used, 1)
                    if m == AFTER_MEAN and stage1:
                        pe.wait_ge(na.rrms_ok, u + 1)
                        norm_mean(na, u + 1)
                    if m == (AFTER_Q if stage2 else AFTER_Q_LAST):
                        pe.wait_ge(a.qsum, t + 1)
                        pe.wait_ge(a.rk_ok, t + 1)
                        mean(b_qk, sum_qk).then_inc(a.q_mm, 1)

            tile_a(0, first=True)
            with pe.Fori(1, LAST - 1) as t:
                tile_a(t)
            tile_a(LAST - 1, stage1=False)
            tile_a(LAST, stage1=False, stage2=False)

            def logits(u):
                pe.wait_ge(nd.h_ok, NC * (u + 1))
                for m in range(NC):
                    ins = nc.tensor.matmul(b_x[0:E, :], gw_t[:, m * E:(m + 1) * E], ch(x_t, m),
                                           start=(m == 0), stop=(m == NC - 1))
                ins.then_inc(nd.logit_mm, 1)

            def logits_to_tokens(u):
                pe.wait_ge(nd.rows_ok, u + 1)
                pe.sem_inc(settled)
                for s in range(NSUB):
                    ins = nc.tensor.transpose(b_x[:, s * E:(s + 1) * E], lg_rows[:, s * P:(s + 1) * P],
                                              ident_t[0:E, 0:E])
                ins.then_inc(nd.lt_mm, 1)

            def gates_to_rows(u):
                pe.wait_ge(nd.gt_ok, u + 1)
                for s in range(NSUB):
                    ins = nc.tensor.transpose(b_x[:, s * P:(s + 1) * P], gates_tok[:, s, :], ident_t[:, :])
                ins.then_inc(nd.tr_mm, 1)

            def hooks(h, s, u):
                if s == h["mean"]:
                    norm_mean(nd, u)
                if s == h["var"]:
                    norm_var(nd, u)
                if s == h["logit"]:
                    logits(u)
                if s == h["top"]:
                    logits_to_tokens(u)
                if s == h["tr"]:
                    gates_to_rows(u)

            def up(p, t, s):
                f, nb = ffn[p], NB[p]
                pe.wait_ge(w_ok, W0[p] + s + 1)
                first = NC * (NT * PASS[p] + t) if s == 0 else None
                if UPS[p] == 2:
                    for half in range(2):
                        o = 2 * s + half
                        if o >= 3:
                            read = f.s_ok if (o - 3) % 2 else f.act_ok
                            pe.wait_ge(read, nb * t + (o - 3) // 2 + 1)
                        from_x(bank[4 + o % 3][:, :], swi_col[s] + half * QKV_W,
                               first if half == 0 else None).then_inc(f.up, 1)
                    return
                if s >= 2:
                    pe.wait_ge(f.act_ok, nb * t + s - 1)
                from_x(bank[4 + s % 2][:, :], moe_col[s], first).then_inc(f.up, 1)
                if s % 2 == 0 and s < N_ROUTED[p]:
                    e = (0 if p == "d" else NB_MOE // 2) + s // 2
                    if s == 0:
                        pe.wait_ge(g_cp, (NT if p == "e" else 0) + t + 1)
                        pe.wait_ge(sel_ok, 3)
                    if s > 0:
                        pe.wait_ge(f.s_ok, nb * t + s)
                    nc.tensor.matmul(bank[6][:, :], sel_t[:, e * P:(e + 1) * P], g_rows[0:2 * E, :],
                                     start=True, stop=True).then_inc(f.gb, 1)

            def down(p, t, s, final=False):
                f, nb = ffn[p], NB[p]
                pe.wait_ge(f.sl_ok, nb * t + s + 1)
                if s == 0:
                    if p == "e":
                        for m in range(NC):
                            ins = nc.tensor.matmul(bank[m][:, :], b2_parts[:, m * P:(m + 1) * P], g_rows[:, :],
                                                   start=True, stop=False)
                        ins.then_inc(f.gb, 1)
                col = swi_col[s] + 2 * QKV_W if UPS[p] == 2 else moe_col[s] + QKV_W
                for m in range(NC):
                    ins = product(bank[m][:, :], s_hi[:, s % 3, :], s_lo[:, s % 3, :], col + m * P,
                                  s == 0 and p != "e", s == nb - 1)
                    if final:
                        ins.then_inc(final_dn, 1)
                if not final:
                    ins.then_inc(f.dn, 1)

            def tile(p, t, last=False):
                for s in range(NB[p] + 2):
                    if s < NB[p]:
                        up(p, t, s)
                    if s >= 2:
                        down(p, t, s - 2, final=last and p == "e" and s == NB[p] + 1)
                    if p == "d" and not last:
                        hooks(HOOKS_D, s, t + 1)
                    if p == "c" and last:
                        hooks(HOOKS_C, s, 0)

            for p in "bcde":
                if p == "c":
                    pe.wait_ge(const_in, 4 * 16)
                if p == "b":
                    pe.wait_ge(a.wv_ok, NC * NT)
                    pe.wait_ge(a.kq_ev, 2 * NC * NT)
                    pe.wait_ge(a.rq_ok, NT)
                else:
                    prev = ffn[{"c": "b", "d": "c", "e": "d"}[p]]
                    nbp = NB[{"c": "b", "d": "c", "e": "d"}[p]]
                    pe.wait_ge(prev.s_ok, nbp * NT)
                with pe.Fori(0, LAST) as t:
                    tile(p, t)
                tile(p, LAST, last=True)

        @block.scalar
        def _(act):
            act.wait_ge(c_in, 16)
            nc.scalar.preload_act_table_set(EXP_LN_SET)
            nc.scalar.activation(c_e[:, :], c_t[:, :], ACT.Exp, scale=-1.0).then_inc(c_exp, 1)

            def rsqrt_seed(dst, square, src, eps, chain, n, seed_done):
                nc.scalar.activation(dst[:, :], src[:, :], ACT.Ln, bias=eps).then_inc(chain, 1)
                act.wait_ge(chain, 2 * n + 1)
                nc.scalar.activation(dst[:, :], dst[:, :], ACT.Exp, scale=-0.5).then_inc(chain, 1)
                act.wait_ge(chain, 2 * n + 2)
                nc.scalar.activation(square[:, :], dst[:, :], ACT.Square).then_inc(seed_done, 1)

            def split(ready, count, scale=1.0, used=None, chunks=range(NC), each=False):
                for m in chunks:
                    act.wait_ge(ready, count + (m + 1 if each else 0))
                    if used is not None:
                        act.wait_ge(a.x_used, used + m + 1)
                    nc.scalar.activation(ch(x_hi, m), ch(x_t, m), ACT.Copy, scale=scale).then_inc(xh_ok, 1)

            def norm_sq(n, src, u):
                for m in range(NC):
                    act.wait_ge(n.d_ok, NC * u + m + 1 if n is na else u + 1)
                    nc.scalar.activation(ch(sq_t, m), ch(src, m), ACT.Square).then_inc(n.dsq_ok, 1)

            def norm_seed(n, u):
                act.wait_ge(n.var_mm, u + 1)
                rsqrt_seed(rs_x, nt_x, b_x, eps_ln, n.ln_ok, u, n.seed_ok)

            def norm_h(n, u, c_vec, s_vec, chunks=range(NC)):
                for m in chunks:
                    act.wait_ge(n.dr_ok, NC * u + m + 1)
                    nc.scalar.activation(ch(x_t, m), ch(x_t, m), ACT.Identity, bias=vec(u, s_vec, m),
                                         scale=vec(u, c_vec, m)).then_inc(n.h_ok, 1)

            def norm_hsq(u, m):
                act.wait_ge(na.h_ok, NC * u + m + 1)
                nc.scalar.activation(ch(sq_t, m), ch(x_t, m), ACT.Square).then_inc(na.hsq_ok, 1)

            def norm_h_hsq(u):
                for m in range(NC):
                    norm_h(na, u, CA, SA, (m,))
                    if m > 0:
                        norm_hsq(u, m - 1)
                norm_hsq(u, NC - 1)

            def norm_rseed(u):
                act.wait_ge(na.rms_mm, u + 1)
                rsqrt_seed(rs_x, nt_x, b_x, eps_rms, na.lnr_ok, u, na.seedr_ok)

            def square_out(m, o, dst, sq, t):
                act.wait_ge(a.mm, (NQKV - 1) * t + o + 1)
                nc.scalar.activation(ch(dst, m), bank[o % 6][:, :], ACT.Copy)
                nc.scalar.activation(ch(sq, m), bank[o % 6][:, :], ACT.Square).then_inc(a.kq_ev, 1)

            def take_rows(v):
                act.wait_ge(mod_mm, v + 1)
                nc.scalar.activation(wmod_bufs[v][0:NB_SEQ, 0:D], bank[v][0:NB_SEQ, :], ACT.Copy).then_inc(mod_row, 1)

            norm_sq(na, x_a, 0)
            take_rows(0)
            norm_seed(na, 0)
            take_rows(1)
            take_rows(2)
            act.wait_ge(mod_ok, 1)
            norm_h_hsq(0)
            take_rows(3)
            norm_rseed(0)
            take_rows(4)
            split(na.n_ok, 0, -0.5, each=True)
            take_rows(5)
            norm_sq(na, x_a, 1)

            def take_k(t, m, tail):
                if tail:
                    act.wait_ge(a.scan_ok, 2 * (NC * (t - 1) + m + 1))
                square_out(m, m, k_t, wv_t, t)

            def take_q(t, m, tail, squares):
                if tail and m % 2 == 0:
                    act.wait_ge(a.y0_ok, 2 * (t - 1) + m // 2 + 1)
                square_out(m, NC + m, q_t, squares, t)

            def seed_k(t):
                act.wait_ge(a.k_mm, t + 1)
                rsqrt_seed(rs_qk, nt_qk, b_qk, eps_rms, a.ln_k, t, a.seed_k)

            def seed_q(t):
                act.wait_ge(a.q_mm, t + 1)
                rsqrt_seed(rs_qk, nt_qk, b_qk, eps_rms, a.ln_q, t, a.seed_q)

            def exp_k(t):
                act.wait_ge(a.kn_ok, t + 1)
                nc.scalar.activation(k_t[:, :], k_t[:, :], ACT.Exp, scale=-0.5).then_inc(a.w_ok, 1)

            def tile_a(t, stage1=True, stage2=True, tail=True):
                u = t + 1
                if stage2:
                    norm_seed(na, u)
                if tail:
                    exp_q(t - 1)
                for m in range(NC):
                    take_k(t, m, tail)
                if stage2:
                    norm_h_hsq(u)
                if tail:
                    seed_y(t - 1)
                seed_k(t)
                if stage2:
                    norm_rseed(u)
                for m in range(NC):
                    take_q(t, m, tail, wv_t if stage2 else sq_t)
                exp_k(t)
                if stage1:
                    norm_sq(na, x_a, u + 1)
                if stage2:
                    split(na.n_ok, NC * u, -0.5, NC * t, each=True)
                seed_q(t)
                if not stage2:
                    split(x_in, 16, 1.0, NC * t)

            def exp_q(t):
                act.wait_ge(a.qn_ok, t + 1)
                nc.scalar.activation(q_t[:, :], q_t[:, :], ACT.Exp, scale=0.5).then_inc(a.e_ok, 1)

            def seed_y(t):
                act.wait_ge(a.den_ok, t + 1)
                nc.scalar.activation(q_t[:, :], wc_t[:, :], ACT.Ln, scale=SEED_SCALE).then_inc(a.ln_y, 1)
                act.wait_ge(a.ln_y, t + 1)
                for half in halves:
                    nc.scalar.activation(q_t[:, half], q_t[:, half], ACT.Exp, scale=-1.0,
                                         bias=seed_shift).then_inc(a.seed_y, 1)

            tile_a(0, tail=False)
            with act.Fori(1, LAST - 1) as t:
                tile_a(t)
            tile_a(LAST - 1, stage1=False)
            tile_a(LAST, stage1=False, stage2=False)
            exp_q(LAST)

            def hooks(h, s, u, back_to):
                if s == h["sq"]:
                    norm_sq(nd, x_t, u)
                if s == h["var"]:
                    nc.scalar.preload_act_table_set(EXP_LN_SET)
                    norm_seed(nd, u)
                if s == h["h"]:
                    norm_h(nd, u, CB, SB)
                if s == h["logit"]:
                    act.wait_ge(nd.logit_mm, u + 1)
                    nc.scalar.activation(lg_rows[:, :], b_x[0:E, :], ACT.Copy).then_inc(nd.rows_ok, 1)
                if s == h["e"]:
                    nc.scalar.preload_act_table_set(EXP_LN_SET)
                    act.wait_ge(nd.top_ok, u + 1)
                    nc.scalar.activation(g2[:, :], m2[:, :], ACT.Exp).then_inc(nd.e_ok, 1)
                if s in (h["var"], h["e"]):
                    nc.scalar.preload_act_table_set(back_to)

            def take_gates(u, first):
                act.wait_ge(nd.tr_mm, u + 1)
                if not first:
                    act.wait_ge(g_st, 16 * u)
                nc.scalar.activation(g_next[:, :], b_x[0:NG, :], ACT.Copy).then_inc(nd.gp_ok, 1)

            def block_(p, t, s):
                f, nb = ffn[p], NB[p]
                act.wait_ge(f.up, UPS[p] * (nb * t + s) + 1)
                if UPS[p] == 2:
                    nc.scalar.activation(act_t[:, s % 2, :], bank[4 + 2 * s % 3][:, :], ACT.Silu).then_inc(f.act_ok, 1)
                else:
                    j = s + (NB_MOE if p == "e" else 0)
                    nc.scalar.activation(act_t[:, s % 2, :], bank[4 + s % 2][:, :], ACT.Gelu,
                                         bias=b1_t[:, j:j + 1]).then_inc(f.act_ok, 1)
                act.wait_ge(f.s_ok, nb * t + s + 1)
                nc.scalar.activation(s_hi[:, s % 3, :], s_t[:, s % 2, :], ACT.Copy).then_inc(f.sh_ok, 1)

            def rows_of_gates(p, t):
                if p == "d":
                    act.wait_ge(nd.gp_ok, t + 1)
                else:
                    act.wait_ge(g_in, 16 * (t + 1))
                nc.scalar.activation(g_rows[:, :], g_next[:, :], ACT.Copy).then_inc(g_cp, 1)

            def tile(p, t, last=False, tail=False):
                f = ffn[p]
                for s in range(NB[p]):
                    block_(p, t, s)
                    if tail and s == 1:
                        nc.scalar.preload_act_table_set(EXP_LN_SET)
                        seed_y(LAST)
                        nc.scalar.preload_act_table_set(SILU_SET)
                    if p == "d" and not last:
                        hooks(HOOKS_D, s, t + 1, GELU_SET)
                    if p == "c" and last:
                        hooks(HOOKS_C, s, 0, SILU_SET)
                if last and p == "e":
                    return
                q, u = (NEXT[p], 0) if last else (p, t + 1)
                act.wait_ge(f.up, UPS[p] * NB[p] * (t + 1))
                if q == "d":
                    split(nd.h_ok, NC * (u + 1))
                    take_gates(u, last)
                else:
                    split(x_in, 16 * (NT * (PASS[q] - 1) + u + 1))
                if q in "de":
                    rows_of_gates(q, u)

            for p in "bcde":
                nc.scalar.preload_act_table_set(SILU_SET if UPS[p] == 2 else GELU_SET)
                if p == "b":
                    tile(p, 0, tail=True)
                if p == "d":
                    act.wait_ge(const_in, 4 * 16)
                with act.Fori(1 if p == "b" else 0, LAST) as t:
                    tile(p, t)
                tile(p, LAST, last=True)

        @block.vector
        def _(dve):
            nc.vector.memset(eps_ln, LN_EPS)
            nc.vector.memset(eps_rms, RMS_EPS)
            nc.vector.memset(seed_shift, math.log(SEED_SCALE))
            nc.vector.memset(mean_w[:, :], 1.0 / D).then_inc(ones_ok, 1)
            nc.vector.memset(carry_kv[:, :], 0.0).then_inc(carry_ok, 1)
            nc.vector.memset(carry_w[:, :], W_EPS).then_inc(carry_ok, 1)
            nc.vector.memset(mod_t[:, :, 6 * NC:6 * NC + 1], 1.0)
            nc.vector.memset(mod_t[:, :, 6 * NC + 1:6 * NC + 2], 0.0).then_inc(keep_ok, 1)
            dve.wait_ge(c_exp, 1)
            nc.vector.tensor_scalar(c_e[:, :], c_e[:, :], 1.0, None, ALU.add).then_inc(setup_v, 1)
            dve.wait_ge(setup_v, 1)
            nc.vector.reciprocal(c_e[:, :], c_e[:, :]).then_inc(setup_v, 1)
            dve.wait_ge(setup_v, 2)
            nc.vector.tensor_tensor(c_t[:, :], c_t[:, :], c_e[:, :], ALU.mult).then_inc(c_silu, 1)
            dve.wait_ge(keep_ok, 1)
            nc.vector.memset(mod_t[:, T_SEQ - 1, 6 * NC:6 * NC + 1], 0.0)
            nc.vector.memset(mod_t[:, T_SEQ - 1, 6 * NC + 1:6 * NC + 2], W_EPS)

            def modulation(half):
                n = 3 * NC * NB_SEQ
                part = mod_raw[:, half * n:(half + 1) * n]
                scale, gain = [part[:, k * n // 3:(k + 1) * n // 3] for k in (1, 2)]
                dve.wait_ge(mod_tr, 3 * half + 3)
                nc.vector.tensor_copy(part, b_qk[:, half * n:(half + 1) * n]).then_inc(mod_cp, 1)
                dve.wait_ge(mod_cp, half + 1)
                k = 2 + 5 * half
                sign = mod_tmp[:, half * n // 3:(half + 1) * n // 3]
                nc.vector.tensor_scalar(scale, scale, -0.5, -0.5, ALU.mult, ALU.add).then_inc(setup_v, 1)
                nc.vector.tensor_scalar(sign, gain, 0.0, 2.0, ALU.is_ge, ALU.mult).then_inc(setup_v, 1)
                dve.wait_ge(setup_v, k + 2)
                nc.vector.tensor_scalar(sign, sign, 1.0, None, ALU.subtract).then_inc(setup_v, 1)
                dve.wait_ge(setup_v, k + 3)
                nc.vector.tensor_tensor(gain, gain, sign, ALU.mult).then_inc(setup_v, 1)
                dve.wait_ge(setup_v, k + 4)
                nc.vector.scalar_tensor_tensor(out=gain, in0=gain, scalar=0.25, in1=sign, op0=ALU.max,
                                               op1=ALU.mult).then_inc(setup_v, 1)
                dve.wait_ge(setup_v, k + 5)
                by_seq = part.rearrange("p (k b o) -> p b o k", b=NB_SEQ, o=1)
                for b in range(NB_SEQ):
                    ins = nc.vector.tensor_copy(
                        mod_t[:, b * T_SEQ:(b + 1) * T_SEQ, half * 3 * NC:(half + 1) * 3 * NC],
                        by_seq[:, b].broadcast_to([P, T_SEQ, 3 * NC]))
                ins.then_inc(mod_ok, 1)

            def newton(y, f, src, eps, chain, n, done):
                nc.vector.scalar_tensor_tensor(out=f[:, :], in0=src[:, :], scalar=eps, in1=f[:, :],
                                               op0=ALU.add, op1=ALU.mult).then_inc(chain, 1)
                dve.wait_ge(chain, n + 1)
                dve.sem_inc(settled)
                nc.vector.scalar_tensor_tensor(out=y[:, :], in0=f[:, :], scalar=3.0, in1=y[:, :],
                                               op0=ALU.subtract, op1=ALU.mult).then_inc(done, 1)

            def split(g, scale=1.0, chunks=range(NC)):
                for m in chunks:
                    dve.wait_ge(xh_ok, g + m + 1)
                    dve.sem_inc(settled)
                    if scale == 1.0:
                        nc.vector.tensor_tensor(ch(x_lo, m), ch(x_t, m), ch(x_hi, m).bitcast(F32),
                                                ALU.subtract).then_inc(xl_ok, 1)
                    else:
                        nc.vector.scalar_tensor_tensor(out=ch(x_lo, m), in0=ch(x_t, m), scalar=scale,
                                                       in1=ch(x_hi, m).bitcast(F32), op0=ALU.mult,
                                                       op1=ALU.subtract).then_inc(xl_ok, 1)

            def norm_d(n, src, u):
                dve.wait_ge(n.mean_mm, u + 1)
                dve.sem_inc(settled)
                if n is nd:
                    nc.vector.tensor_tensor(rows(src), rows(src), over_chunks(b_x), ALU.subtract).then_inc(n.d_ok, 1)
                    return
                for m in range(NC):
                    nc.vector.tensor_tensor(ch(src, m), ch(src, m), b_x[:, :], ALU.subtract).then_inc(n.d_ok, 1)

            def norm_rstd(n, u):
                dve.wait_ge(n.seed_ok, u + 1)
                dve.sem_inc(settled)
                newton(rs_x, nt_x, b_x, LN_EPS, n.newton, u, n.rstd_ok)

            def norm_dr(n, src, u):
                dve.wait_ge(n.rstd_ok, u + 1)
                dve.sem_inc(settled)
                for m in range(NC):
                    nc.vector.tensor_tensor(ch(x_t, m), ch(src, m), rs_x[:, :], ALU.mult).then_inc(n.dr_ok, 1)

            def norm_residual(u):
                dve.wait_ge(r_in, 16 * (u + 1))
                dve.sem_inc(settled)
                for m in range(NC):
                    dve.wait_ge(na.h_ok, NC * u + m + 1)
                    dve.sem_inc(settled)
                    nc.vector.scalar_tensor_tensor(out=ch(r_t, m), in0=ch(x_t, m), scalar=vec(u, GA, m),
                                                   in1=ch(r_t, m), op0=ALU.mult, op1=ALU.add).then_inc(na.r_ok, 1)

            def norm_n(u):
                dve.wait_ge(na.seedr_ok, u + 1)
                dve.sem_inc(settled)
                newton(rs_x, nt_x, b_x, RMS_EPS, na.newtonr, u, na.rrms_ok)
                dve.wait_ge(na.rrms_ok, u + 1)
                dve.sem_inc(settled)
                dve.wait_ge(na.r_ok, NC * (u + 1))
                dve.sem_inc(settled)
                for m in range(NC):
                    nc.vector.tensor_tensor(ch(x_t, m), ch(x_t, m), rs_x[:, :], ALU.mult).then_inc(na.n_ok, 1)

            dve.wait_ge(xa_in, 16)
            dve.wait_ge(na.mean_mm, 1)
            for m in range(NC):
                nc.vector.tensor_tensor(ch(x_a, m), ch(x_a, m), bank[5][:, :],
                                        ALU.subtract).then_inc(na.d_ok, 1)
            norm_rstd(na, 0)
            norm_dr(na, x_a, 0)
            modulation(0)
            norm_residual(0)
            norm_n(0)
            split(0, -0.5)
            modulation(1)
            norm_d(na, x_a, 1)
            dve.wait_ge(mod_ok, 2)

            def scans(t, first=False):
                if first:
                    dve.wait_ge(carry_ok, 2)
                else:
                    dve.wait_ge(y_st, 16 * t)
                    dve.sem_inc(settled)
                    dve.wait_ge(a.carry, 2 * t)
                    dve.sem_inc(settled)
                for m in range(NC):
                    dve.wait_ge(a.wv_ok, NC * t + m + 1)
                    dve.sem_inc(settled)
                    nc.vector.tensor_tensor_scan(ch(kv_t, m), ch(wv_t, m), ch(wv_t, m), carry_kv[:, m:m + 1],
                                                 ALU.add, ALU.bypass).then_inc(a.scan_ok, 1)
                    nc.vector.tensor_tensor_scan(ch(wc_t, m), ch(k_t, m), ch(k_t, m), carry_w[:, m:m + 1],
                                                 ALU.add, ALU.bypass).then_inc(a.scan_ok, 1)
                dve.wait_ge(a.scan_ok, 2 * NC * (t + 1))
                dve.sem_inc(settled)
                keep = mod_t[:, t, 6 * NC:6 * NC + 1]
                fresh = mod_t[:, t, 6 * NC + 1:6 * NC + 2]
                nc.vector.tensor_scalar(carry_kv[:, :], rows(kv_t)[:, :, TT - 1], keep, None,
                                        ALU.mult).then_inc(a.carry, 1)
                nc.vector.tensor_scalar(carry_w[:, :], rows(wc_t)[:, :, TT - 1], keep, fresh,
                                        ALU.mult, ALU.add).then_inc(a.carry, 1)

            def denominator(t):
                dve.wait_ge(a.carry, 2 * t + 2)
                dve.sem_inc(settled)
                dve.wait_ge(a.e_ok, t + 1)
                dve.sem_inc(settled)
                nc.vector.scalar_tensor_tensor(out=wc_t[:, :], in0=q_t[:, :], scalar=1.0, in1=wc_t[:, :],
                                               op0=ALU.add, op1=ALU.mult).then_inc(a.den_ok, 1)

            def tail_0(t):
                for k, half in enumerate(halves):
                    dve.wait_ge(a.seed_y, 2 * t + k + 1)
                    dve.sem_inc(settled)
                    nc.vector.tensor_tensor(wc_t[:, half], wc_t[:, half], q_t[:, half], ALU.mult)
                    nc.vector.tensor_tensor(kv_t[:, half], kv_t[:, half], q_t[:, half], ALU.mult).then_inc(a.y0_ok, 1)

            def tail_1(t):
                dve.wait_ge(a.y0_ok, 2 * (t + 1))
                dve.sem_inc(settled)
                nc.vector.scalar_tensor_tensor(out=kv_t[:, :], in0=wc_t[:, :], scalar=2.0, in1=kv_t[:, :],
                                               op0=ALU.subtract, op1=ALU.mult, reverse0=True).then_inc(a.y_ok, 1)

            def newton_k(t):
                dve.wait_ge(a.seed_k, t + 1)
                dve.sem_inc(settled)
                newton(rs_qk, nt_qk, b_qk, RMS_EPS, a.newton, 2 * t, a.rk_ok)

            def newton_q(t):
                dve.wait_ge(a.seed_q, t + 1)
                dve.sem_inc(settled)
                newton(rs_qk, nt_qk, b_qk, RMS_EPS, a.newton, 2 * t + 1, a.rq_ok)

            def k_times_v(t, m, stage2):
                if m == 0:
                    if stage2:
                        dve.wait_ge(a.qsum, t + 1)
                        dve.sem_inc(settled)
                    dve.wait_ge(a.w_ok, t + 1)
                    dve.sem_inc(settled)
                if m < NC - 1:
                    dve.wait_ge(a.mm, (NQKV - 1) * t + 2 * NC + m + 1)
                else:
                    dve.wait_ge(a.x_used, NC * (t + 1))
                dve.sem_inc(settled)
                nc.vector.tensor_tensor(ch(wv_t, m), ch(k_t, m), bank[(2 * NC + m) % 6][:, :],
                                        ALU.mult).then_inc(a.wv_ok, 1)

            def tile_a(t, stage1=True, stage2=True, tail=True):
                u = t + 1
                if tail:
                    scans(t - 1, first=isinstance(t, int) and t == 1)
                if stage2:
                    norm_rstd(na, u)
                    dve.wait_ge(xl_ok, NC * u)
                    dve.sem_inc(settled)
                    norm_dr(na, x_a, u)
                if tail:
                    denominator(t - 1)
                if stage2:
                    norm_residual(u)
                if tail:
                    tail_0(t - 1)
                newton_k(t)
                if stage2:
                    norm_n(u)
                if stage1:
                    norm_d(na, x_a, u + 1)
                if tail:
                    tail_1(t - 1)
                if stage2:
                    split(NC * u, -0.5)
                k_times_v(t, 0, stage2)
                newton_q(t)
                for m in range(1, NC):
                    k_times_v(t, m, stage2)

            tile_a(0, tail=False)
            tile_a(1)
            with dve.Fori(2, LAST - 1) as t:
                tile_a(t)
            tile_a(LAST - 1, stage1=False)
            tile_a(LAST, stage1=False, stage2=False)
            split(NC * NT)
            scans(LAST)
            denominator(LAST)

            GCH = 12

            def gating(u):
                n = [GCH * u]

                def then(ins):
                    n[0] = n[0] + 1
                    ins.then_inc(nd.gate_chain, 1)
                    dve.wait_ge(nd.gate_chain, n[0])
                    dve.sem_inc(settled)

                def first_max(onehot, src, top):
                    then(nc.vector.reduce_max(top[:, :], src[:, :, :], axis=AX_X))
                    then(nc.vector.tensor_tensor(eq[:, :, :], src[:, :, :], wide(top), ALU.is_equal))
                    then(nc.vector.tensor_tensor(eq[:, :, :], eq[:, :, :], ranks, ALU.mult))
                    then(nc.vector.reduce_max(fst[:, :], eq[:, :, :], axis=AX_X))
                    then(nc.vector.tensor_tensor(onehot[:, :, :], eq[:, :, :], wide(fst), ALU.is_equal))

                dve.wait_ge(nd.lt_mm, u + 1)
                dve.sem_inc(settled)
                then(nc.vector.tensor_copy(lg[:, :, :], b_x[:, 0:NSUB * E].rearrange("p (s e) -> p s e", s=NSUB)))
                first_max(top1, lg, m1)
                then(nc.vector.scalar_tensor_tensor(out=lg2[:, :, :], in0=top1[:, :, :], scalar=-3.0e38,
                                                    in1=lg[:, :, :], op0=ALU.mult, op1=ALU.add))
                first_max(top2, lg2, m2)
                nc.vector.tensor_tensor(m2[:, :], m2[:, :], m1[:, :], ALU.subtract).then_inc(nd.top_ok, 1)

            def gates(u):
                k = [0]

                def then(ins):
                    k[0] += 1
                    ins.then_inc(gate_fin, 1)
                    dve.wait_ge(gate_fin, 7 * u + k[0])
                    dve.sem_inc(settled)

                dve.wait_ge(nd.e_ok, u + 1)
                dve.sem_inc(settled)
                then(nc.vector.tensor_scalar(g1[:, :], g2[:, :], 1.0, None, ALU.add))
                then(nc.vector.reciprocal(g1[:, :], g1[:, :]))
                then(nc.vector.tensor_tensor(g2[:, :], g2[:, :], g1[:, :], ALU.mult))
                then(nc.vector.tensor_tensor(top1[:, :, :], top1[:, :, :], wide(g1), ALU.mult))
                then(nc.vector.tensor_tensor(top2[:, :, :], top2[:, :, :], wide(g2), ALU.mult))
                then(nc.vector.tensor_tensor(top1[:, :, :], top1[:, :, :], top2[:, :, :], ALU.add))
                then(nc.vector.tensor_copy(gate_cols[:, :, :, 0:E].bitcast(F32R), top1_twice))
                nc.vector.tensor_tensor(gate_cols[:, :, :, E:2 * E], top1_twice, gate_cols[:, :, :, 0:E],
                                        ALU.subtract).then_inc(nd.gt_ok, 1)

            gate_cols = gates_tok[:, :, 0:2 * AGAIN].rearrange("p s (k c) -> p s k c", k=2)
            top1_twice = top1[:, :, :].rearrange("p s (k e) -> p s k e", k=1).broadcast_to([P, NSUB, 2, E])

            def wide(t):
                return t[:, :].rearrange("p (s o) -> p s o", o=1).broadcast_to([P, NSUB, E])

            ranks = rank_t[:, :].rearrange("p (o e) -> p o e", o=1).broadcast_to([P, NSUB, E])

            def hooks(h, s, u):
                if s == h["mean"]:
                    norm_d(nd, x_t, u)
                if s == h["var"]:
                    norm_rstd(nd, u)
                    norm_dr(nd, x_t, u)
                if s == h["top"]:
                    gating(u)
                if s == h["e"]:
                    gates(u)

            def block_(p, t, s):
                f, nb = ffn[p], NB[p]
                routed = s < N_ROUTED[p]
                if UPS[p] == 2:
                    dve.wait_ge(f.up, 2 * (nb * t + s) + 2)
                    dve.sem_inc(settled)
                dve.wait_ge(f.act_ok, nb * t + s + 1)
                dve.sem_inc(settled)
                if UPS[p] == 2:
                    other = bank[4 + (2 * s + 1) % 3][:, :]
                elif routed:
                    per_tile = N_ROUTED[p] // 2 + (1 if p == "e" else 0)
                    dve.wait_ge(f.gb, per_tile * t + s // 2 + 1 + (1 if p == "e" and s >= 4 else 0))
                    dve.sem_inc(settled)
                    other = bank[6][:, :]
                if UPS[p] == 2 or routed:
                    nc.vector.tensor_tensor(s_t[:, s % 2, :], act_t[:, s % 2, :], other, ALU.mult).then_inc(f.s_ok, 1)
                else:
                    nc.vector.tensor_copy(s_t[:, s % 2, :], act_t[:, s % 2, :]).then_inc(f.s_ok, 1)
                dve.wait_ge(f.sh_ok, nb * t + s + 1)
                dve.sem_inc(settled)
                nc.vector.tensor_tensor(s_lo[:, s % 3, :], s_t[:, s % 2, :], s_hi[:, s % 3, :].bitcast(F32),
                                        ALU.subtract).then_inc(f.sl_ok, 1)

            def tile(p, t, last=False, tail=False):
                f, nb = ffn[p], NB[p]
                for s in range(nb):
                    block_(p, t, s)
                    if tail and s == 1:
                        tail_0(LAST)
                    if tail and s == 2:
                        tail_1(LAST)
                    if p == "d" and not last:
                        hooks(HOOKS_D, s, t + 1)
                    if p == "c" and last:
                        hooks(HOOKS_C, s, 0)
                if not (last and p == "e"):
                    q, u = (NEXT[p], 0) if last else (p, t + 1)
                    split(NC * (NT * PASS[q] + u))
                final = last and p == "e"
                if not final:
                    dve.wait_ge(f.dn, nb * (t + 1))
                    dve.sem_inc(settled)
                dve.wait_ge(r_in, 16 * (NT * PASS[p] + t + 1))
                dve.sem_inc(settled)
                for m in range(NC):
                    if final:
                        dve.wait_ge(final_dn, m + 1)
                    nc.vector.scalar_tensor_tensor(out=ch(r_t, m), in0=bank[m][:, :], scalar=vec(t, GAIN[p], m),
                                                   in1=ch(r_t, m), op0=ALU.mult, op1=ALU.add).then_inc(f.ev_ok, 1)

            for p in "bcde":
                if p == "b":
                    tile(p, 0, tail=True)
                    dve.wait_ge(y_st, 16 * NT)
                    dve.wait_ge(const_in, 4 * 16)
                    nc.vector.memset(gates_tok[:, :, :], 0.0).then_inc(ones_ok, 1)
                    dve.wait_ge(ones_ok, 2)
                    for first in (0, AGAIN):
                        nc.vector.memset(gates_tok[:, :, first + ONES:first + ONES + 1], 1.0).then_inc(ones_ok, 1)
                with dve.Fori(1 if p == "b" else 0, LAST) as t:
                    tile(p, t)
                tile(p, LAST, last=True)


def kernel(**inputs):
    import concourse.bacc as bacc
    import numpy as np
    from concourse.bass_utils import run_bass_kernel_spmd

    x = np.ascontiguousarray(inputs["L0_attn_x"])
    B, S, D = x.shape
    nc_, nt = D // P, B * S // TT
    E, _, H = inputs["L0_ffn_w1"].shape

    def blocks(w, rows_, cols):
        return np.asarray(w).reshape(rows_ // P, P, cols // P, P).transpose(2, 0, 1, 3)

    w_qkv = blocks(np.asarray(inputs["L0_attn_w_qkv"]).T, D, 3 * D)
    w_qkv = np.concatenate([w_qkv[nc_:2 * nc_], w_qkv[0:nc_], w_qkv[2 * nc_:]])
    w_qkv = w_qkv.reshape(nc_, 3 * nc_, P, P).transpose(0, 2, 1, 3).reshape(nc_, P, 3 * nc_ * P)
    swi = np.asarray(inputs["L0_attn_w_swiglu"])
    F = swi.shape[0] // 2
    up = blocks(swi.T, D, 2 * F)
    down = np.asarray(inputs["L0_attn_w_out"]).T.reshape(F // P, P, nc_, P).transpose(0, 2, 1, 3)
    w_swi = np.concatenate([up[F // P:], up[:F // P], down], axis=1)
    w_swi = w_swi.transpose(0, 2, 1, 3).reshape(F // P, P, 3 * nc_ * P)
    w1 = np.concatenate([blocks(w, D, H) for w in np.asarray(inputs["L0_ffn_w1"])]
                        + [blocks(inputs["L0_ffn_shared_w1"], D, D)])
    w2 = np.concatenate([np.asarray(inputs["L0_ffn_w2"]).reshape(E * H, D), np.asarray(inputs["L0_ffn_shared_w2"])])
    w2 = w2.reshape(-1, P, nc_, P).transpose(0, 2, 1, 3)
    w_moe = np.concatenate([w1, w2], axis=1).transpose(0, 2, 1, 3).reshape(-1, P, 2 * nc_ * P)
    b1 = np.concatenate([np.asarray(inputs["L0_ffn_b1"]).reshape(-1), np.asarray(inputs["L0_ffn_shared_b1"])])
    b2 = np.asarray(inputs["L0_ffn_b2"])
    b2 = np.concatenate([b2, b2, np.asarray(inputs["L0_ffn_shared_b2"])[None]])
    b2 = np.concatenate([b2, np.zeros((32 - 2 * E - 1, D), np.float32), b2])
    c = np.asarray(inputs["L0_c"]).reshape(B, nc_, P).transpose(2, 1, 0).reshape(P, nc_ * B)
    wmod = np.asarray(inputs["L0_wmod"]).reshape(nc_, P, 6, D).transpose(2, 1, 0, 3).reshape(6, P, nc_ * D)
    gate_w = np.asarray(inputs["L0_ffn_gate_w"]).reshape(nc_, P, E).transpose(1, 0, 2).reshape(P, nc_ * E)
    arrays = {
        "x": x.reshape(nt, TT, nc_, P).transpose(0, 3, 2, 1).reshape(nt, P, nc_ * TT),
        "c": c, "wmod": wmod, "w_qkv": w_qkv, "w_swi": w_swi, "w_moe": w_moe,
        "b1": b1.reshape(-1, P).T, "b2": b2, "gate_w": gate_w,
        "select": np.repeat(np.concatenate([np.eye(E), np.eye(E)]), P, axis=1).astype(np.float32),
        "ident": np.eye(P, dtype=np.float32),
        "rank": np.tile(np.arange(E, 0, -1, dtype=np.float32), (P, 1)),
    }
    arrays = {k: np.ascontiguousarray(v) for k, v in arrays.items()}
    nc = bacc.Bacc("TRN2", target_bir_lowering=False, num_devices=1)
    args = [nc.dram_tensor(k, v.shape, mybir.dt.from_np(v.dtype), kind="ExternalInput").ap()
            for k, v in arrays.items()]
    out = nc.dram_tensor("out", (nt, P, nc_ * TT), F32, kind="ExternalOutput").ap()
    build(nc, *args, out)
    r = run_bass_kernel_spmd(nc, [arrays], core_ids=[0])
    got = np.asarray(r.results[0]["out"]).reshape(nt, P, nc_, TT).transpose(0, 3, 2, 1)
    return np.ascontiguousarray(got).reshape(B, S, D)
```
